# Optimizing a Trainium2 kernel written in Bass

```python
import numpy as np
import jax
import jax.numpy as jnp

def _softmax(x, axis=-1):
    return jax.nn.softmax(x, axis=axis)

def _gelu(x):
    return jax.nn.gelu(x, approximate=True)

def _silu(x):
    return jax.nn.silu(x)

def _sigmoid(x):
    return jax.nn.sigmoid(x)

def _layernorm(x, axis=-1, eps=1e-05):
    m = jnp.mean(x, axis=axis, keepdims=True)
    v = jnp.var(x, axis=axis, keepdims=True)
    return (x - m) / jnp.sqrt(v + eps)

def _scatter_add(tgt, idx, src, axis=0):
    return tgt.at[idx].add(src)

def _segment_sum(src, seg, n):
    return jax.ops.segment_sum(src, seg, n)
kernel_name = 'mk_vit_tower_postln_d1_tok_img512_r4_aa7d07'

def setup_inputs(seed: int=0):
    np.random.seed(seed)
    _w = jnp.asarray

    def _rec_inputs():
        import jax
        import jax.numpy as jnp
        _rk = jax.random.key(seed)
        x = -0.000477451 + 1.00034 * jax.random.normal(jax.random.fold_in(_rk, 1), (8, 32, 32, 29), jnp.float32)
        return x
    x = _rec_inputs()

    def _L0_tok_setup():
        import jax, jax.numpy as jnp
        import numpy as np
        import math
        H, W_DIM, D_MODEL, B = (32, 32, 128, 128)
        F_TOTAL = 29
        SEQ_LEN = H * W_DIM

        def make_pe(seq_len: int, d_model: int) -> jnp.ndarray:
            position = np.arange(seq_len, dtype=np.float32)[:, None]
            div_term = np.exp(np.arange(0, d_model, 2, dtype=np.float32) * (-math.log(10000.0) / d_model))
            pe = np.zeros((seq_len, d_model), dtype=np.float32)
            pe[:, 0::2] = np.sin(position * div_term)
            pe[:, 1::2] = np.cos(position * div_term)
            return jnp.asarray(pe)
        key = jax.random.key(seed)
        k1, k2 = jax.random.split(key)
        state_tensor = jax.random.normal(k1, (B, H, W_DIM, F_TOTAL), dtype=jnp.float32)
        W = jax.random.normal(k2, (F_TOTAL, D_MODEL), dtype=jnp.float32) * 0.05
        return {'state_tensor': state_tensor, 'W': W}
    _L0_tok_all = _L0_tok_setup()
    _L0_tok_in = {k: v for k, v in _L0_tok_all.items() if k in ('W',)}
    del _L0_tok_all

    def _L0_attn_setup():
        import jax, jax.numpy as jnp
        import numpy as np
        B, S, IN, HD, H = (2, 512, 128, 32, 16)
        key = jax.random.key(seed)
        ks = jax.random.split(key, 9)
        sc = 0.02
        return {'x': jax.random.normal(ks[0], (B, S, IN), jnp.float32), 'Wl': jax.random.normal(ks[1], (H, IN, IN), jnp.float32) * sc, 'bl': jax.random.normal(ks[2], (H, IN), jnp.float32) * sc, 'Wq': jax.random.normal(ks[3], (H, IN, HD), jnp.float32) * sc, 'Wk': jax.random.normal(ks[4], (H, IN, HD), jnp.float32) * sc, 'Wv': jax.random.normal(ks[5], (H, IN, HD), jnp.float32) * sc, 'Wo': jax.random.normal(ks[6], (IN, H * HD), jnp.float32) * sc, 'bo': jax.random.normal(ks[7], (IN,), jnp.float32) * sc}
    _L0_attn_all = _L0_attn_setup()
    _L0_attn_in = {k: v for k, v in _L0_attn_all.items() if k in ('Wl', 'bl', 'Wq', 'Wk', 'Wv', 'Wo', 'bo')}
    del _L0_attn_all

    def _L0_ffn_setup():
        import jax, jax.numpy as jnp
        import numpy as np
        from jax import lax
        N_HEADS = 8
        D_KEYS = 128
        HALF = D_KEYS // 2
        N_KEYS = 64
        TOP_K = 8
        D_MODEL = 128

        def _forward(queries, Wq, bq, keys, w_down, w_up):
            N, T, D = queries.shape
            x = queries.reshape(-1, D)
            q = (x @ Wq + bq).reshape(-1, N_HEADS, D_KEYS)
            q1, q2 = (q[..., :HALF], q[..., HALF:])
            s1 = jnp.einsum('bhc,hnc->bhn', q1, keys[:, 0])
            s2 = jnp.einsum('bhc,hnc->bhn', q2, keys[:, 1])
            s1t, i1 = lax.top_k(s1, TOP_K)
            s2t, i2 = lax.top_k(s2, TOP_K)
            all_scores = (s1t[..., :, None] + s2t[..., None, :]).reshape(-1, N_HEADS, TOP_K * TOP_K)
            all_idx = (i1[..., :, None] * N_KEYS + i2[..., None, :]).reshape(-1, N_HEADS, TOP_K * TOP_K)
            scores, best = lax.top_k(all_scores, TOP_K)
            indices = jnp.take_along_axis(all_idx, best, axis=-1)
            w_d = w_down[indices]
            w_u = w_up[indices]
            inner = jnp.einsum('bd,bhkd->bhk', x, w_d)
            vals = jax.nn.relu(inner) * jax.nn.softmax(scores, axis=-1)
            out = jnp.einsum('bhk,bhkd->bd', vals, w_u)
            return out.reshape(N, T, D)
        key = jax.random.key(seed)
        ks = jax.random.split(key, 6)
        N, T = (2, 256)
        queries = jax.random.normal(ks[0], (N, T, D_MODEL), dtype=jnp.float32)
        Wq = jax.random.normal(ks[1], (D_MODEL, N_HEADS * D_KEYS), dtype=jnp.float32) / np.sqrt(D_MODEL)
        bq = jnp.zeros((N_HEADS * D_KEYS,), dtype=jnp.float32)
        bound = 1.0 / np.sqrt(HALF)
        keys = jax.random.uniform(ks[2], (N_HEADS, 2, N_KEYS, HALF), dtype=jnp.float32, minval=-bound, maxval=bound)
        w_down = jax.random.normal(ks[3], (N_KEYS * N_KEYS, D_MODEL), dtype=jnp.float32) * 0.02
        w_up = jax.random.normal(ks[4], (N_KEYS * N_KEYS, D_MODEL), dtype=jnp.float32) * 0.02
        return {'queries': queries, 'Wq': Wq, 'bq': bq, 'keys': keys, 'w_down': w_down, 'w_up': w_up}
    _L0_ffn_all = _L0_ffn_setup()
    _L0_ffn_in = {k: v for k, v in _L0_ffn_all.items() if k in ('Wq', 'bq', 'keys', 'w_down', 'w_up')}
    del _L0_ffn_all
    return {'x': x, 'L0_tok_W': _L0_tok_in['W'], 'L0_attn_Wl': _L0_attn_in['Wl'], 'L0_attn_bl': _L0_attn_in['bl'], 'L0_attn_Wq': _L0_attn_in['Wq'], 'L0_attn_Wk': _L0_attn_in['Wk'], 'L0_attn_Wv': _L0_attn_in['Wv'], 'L0_attn_Wo': _L0_attn_in['Wo'], 'L0_attn_bo': _L0_attn_in['bo'], 'L0_ffn_Wq': _L0_ffn_in['Wq'], 'L0_ffn_bq': _L0_ffn_in['bq'], 'L0_ffn_keys': _L0_ffn_in['keys'], 'L0_ffn_w_down': _L0_ffn_in['w_down'], 'L0_ffn_w_up': _L0_ffn_in['w_up']}

def reference(x, L0_tok_W, L0_attn_Wl, L0_attn_bl, L0_attn_Wq, L0_attn_Wk, L0_attn_Wv, L0_attn_Wo, L0_attn_bo, L0_ffn_Wq, L0_ffn_bq, L0_ffn_keys, L0_ffn_w_down, L0_ffn_w_up):
    import jax
    import jax.numpy as jnp

    def _L0_tok_ref(state_tensor, W):
        import jax, jax.numpy as jnp
        import numpy as np
        import math
        H, W_DIM, D_MODEL, B = (32, 32, 128, 128)
        F_TOTAL = 29
        SEQ_LEN = H * W_DIM

        def make_pe(seq_len: int, d_model: int) -> jnp.ndarray:
            position = np.arange(seq_len, dtype=np.float32)[:, None]
            div_term = np.exp(np.arange(0, d_model, 2, dtype=np.float32) * (-math.log(10000.0) / d_model))
            pe = np.zeros((seq_len, d_model), dtype=np.float32)
            pe[:, 0::2] = np.sin(position * div_term)
            pe[:, 1::2] = np.cos(position * div_term)
            return jnp.asarray(pe)
        b, h, w, f = state_tensor.shape
        s = h * w
        x = state_tensor.reshape(b, s, f)
        emb = jnp.einsum('bsf,fd->bsd', x, W)
        pe = make_pe(s * 2, W.shape[1])[:s]
        return emb + pe[None, :, :]

    def _L0_attn_ref(x, Wl, bl, Wq, Wk, Wv, Wo, bo):
        import jax, jax.numpy as jnp
        import numpy as np
        B, S, IN, HD, H = (2, 512, 128, 32, 16)
        b, s, _ = x.shape
        h, _, hd = Wq.shape
        xh = jnp.einsum('bsi,hoi->bhso', x, Wl) + bl[None, :, None, :]
        Q = jnp.einsum('bhsi,hid->bhsd', xh, Wq)
        K = jnp.einsum('bhsi,hid->bhsd', xh, Wk)
        V = jnp.einsum('bhsi,hid->bhsd', xh, Wv)
        scores = jnp.einsum('bhsd,bhtd->bhst', Q, K)
        causal = jnp.triu(jnp.ones((s, s), dtype=bool), k=1)
        scores = jnp.where(causal[None, None], -jnp.inf, scores)
        A = jax.nn.softmax(scores, axis=-1)
        F = jnp.einsum('bhst,bhtd->bhsd', A, V)
        cat = jnp.transpose(F, (0, 2, 1, 3)).reshape(b, s, h * hd)
        return cat @ Wo.T + bo

    def _L0_ffn_ref(queries, Wq, bq, keys, w_down, w_up):
        import jax, jax.numpy as jnp
        import numpy as np
        from jax import lax
        N_HEADS = 8
        D_KEYS = 128
        HALF = D_KEYS // 2
        N_KEYS = 64
        TOP_K = 8
        D_MODEL = 128

        def _forward(queries, Wq, bq, keys, w_down, w_up):
            N, T, D = queries.shape
            x = queries.reshape(-1, D)
            q = (x @ Wq + bq).reshape(-1, N_HEADS, D_KEYS)
            q1, q2 = (q[..., :HALF], q[..., HALF:])
            s1 = jnp.einsum('bhc,hnc->bhn', q1, keys[:, 0])
            s2 = jnp.einsum('bhc,hnc->bhn', q2, keys[:, 1])
            s1t, i1 = lax.top_k(s1, TOP_K)
            s2t, i2 = lax.top_k(s2, TOP_K)
            all_scores = (s1t[..., :, None] + s2t[..., None, :]).reshape(-1, N_HEADS, TOP_K * TOP_K)
            all_idx = (i1[..., :, None] * N_KEYS + i2[..., None, :]).reshape(-1, N_HEADS, TOP_K * TOP_K)
            scores, best = lax.top_k(all_scores, TOP_K)
            indices = jnp.take_along_axis(all_idx, best, axis=-1)
            w_d = w_down[indices]
            w_u = w_up[indices]
            inner = jnp.einsum('bd,bhkd->bhk', x, w_d)
            vals = jax.nn.relu(inner) * jax.nn.softmax(scores, axis=-1)
            out = jnp.einsum('bhk,bhkd->bd', vals, w_u)
            return out.reshape(N, T, D)
        return _forward(queries, Wq, bq, keys, w_down, w_up)
    h = _L0_tok_ref(x, L0_tok_W)
    h = _layernorm(h + _L0_attn_ref(h, L0_attn_Wl, L0_attn_bl, L0_attn_Wq, L0_attn_Wk, L0_attn_Wv, L0_attn_Wo, L0_attn_bo), axis=-1)
    h = _layernorm(h + _L0_ffn_ref(h, L0_ffn_Wq, L0_ffn_bq, L0_ffn_keys, L0_ffn_w_down, L0_ffn_w_up), axis=-1)
    return h

_drawn_inputs = setup_inputs


def setup_inputs(seed=0):
    import zlib

    import numpy as np

    out = dict(_drawn_inputs(seed))
    spreads = {'L0_ffn_bq': (0.0, 0.8)}
    factors = {'L0_attn_Wl': 4.397,
     'L0_attn_bl': 8.0,
     'L0_attn_Wq': 8.0,
     'L0_attn_Wk': 8.0,
     'L0_attn_Wv': 3.592,
     'L0_attn_Wo': 3.598,
     'L0_ffn_Wq': 8.0,
     'L0_ffn_keys': 8.0,
     'L0_ffn_w_down': 8.0,
     'L0_ffn_w_up': 8.0}
    for name, (base, spread) in spreads.items():
        noise = np.random.default_rng([zlib.crc32(name.encode()), seed]).standard_normal(out[name].shape)
        drawn = base * np.exp(spread * noise) if base else spread * noise
        out[name] = jnp.asarray(drawn.astype(out[name].dtype))
    for name, factor in factors.items():
        out[name] = (out[name] * factor).astype(out[name].dtype)
    return out
```

```python
from contextlib import ExitStack

import concourse.bass as bass
import numpy as np
from concourse import mybir
from concourse.alu_op_type import AluOpType as ALU

F32 = mybir.dt.float32
BF16 = mybir.dt.bfloat16
F16 = mybir.dt.float16
I32 = mybir.dt.int32
U32 = mybir.dt.uint32
ACT = mybir.ActivationFunctionType
AX_X = mybir.AxisListType.X

P = 128
B, SEQ, FEAT, D = 8, 1024, 29, 128
HEADS, HD = 16, 32
HG = 4
GROUPS = HEADS // HG
QT = SEQ // P
CHUNK = 512
EPS = 1e-5
EXACT = 96
PARTS = 3

Q_STACK = ((0, 1, 0), (1, 2, 0))
K_STACK = ((0, 0, 1), (1, 0, 2))

UNITS = [(c, kt) for c in range(SEQ // CHUNK) for kt in range((c + 1) * CHUNK // P)]
PIECES = [(qt, tuple(range(h, h + n))) for qt in range(QT)
          for n in ((4, 4, 2, 2, 1, 1, 1, 1)[qt],) for h in range(0, HG, n)]
PIECE_SLOTS = {5: 4, 6: 4, 7: 4, 8: 4, 9: 3, 10: 3}


def pieces_at(u):
    first = sum(n for v, n in PIECE_SLOTS.items() if v < u)
    return PIECES[first:first + PIECE_SLOTS.get(u, 0)]


def unit_span(c, kt):
    q0 = max(CHUNK * c, P * kt)
    return q0, CHUNK * (c + 1) - q0


NEXT_GROUP = ["q", "k", "v"] + [("max",) + p for p in PIECES] + ["rows"]
PROLOGUE_USES = ["fold0", "fold1", "bias", "outbias", "embed"] + NEXT_GROUP


def iteration_uses(last):
    uses = []
    for g in range(GROUPS):
        if g == GROUPS - 1:
            uses += [] if last else [(g, "embed")] + [(g, x) for x in NEXT_GROUP]
        else:
            uses += [(g, x) for x in NEXT_GROUP]
    return uses + [(GROUPS - 1, "out")]


def attention(nc, ins, h1, outer):
    ctx = outer.enter_context(ExitStack())

    def sb(name, shape, dt):
        return ctx.enter_context(nc.sbuf_tensor(name, shape, dt))

    def sem(name):
        return ctx.enter_context(nc.semaphore(name))

    wide = [ctx.enter_context(nc.psum_tensor(f"wide{i}", [P, SEQ], F32)) for i in range(2)]
    score = [ctx.enter_context(nc.psum_tensor(f"score{i}", [P, CHUNK], F32)) for i in range(2)]
    mixed = ctx.enter_context(nc.psum_tensor("mixed", [P, CHUNK], F32))
    total = ctx.enter_context(nc.psum_tensor("total", [P, CHUNK], F32))

    blT = sb("blT", [P, HEADS], F32)
    wqkv = sb("wqkv", [P, 3, HEADS * HD], F32)
    woT = sb("woT", [P, GROUPS, D], F32)
    bo = sb("bo", [P, D], F32)
    bias = sb("bias", [P, 3 * GROUPS], F32)
    wtok = sb("wtok", [FEAT, D], F32)
    cst = sb("cst", [P, 3, P], F32)
    ident = cst[:, 0, :]
    cst16 = sb("cst16", [P, 3, P], BF16)
    ident16, above, below = cst16[:, 0, :], cst16[:, 1, :], cst16[:, 2, :]
    ones = sb("ones", [P, HD], F32)
    peT = sb("peT", [P, SEQ], F32)
    peb = sb("peb", [P, QT, D], F32)

    x_next = sb("x_next", [FEAT, SEQ], F32)
    x_here = sb("x_here", [FEAT, SEQ], F32)
    h0T = sb("h0T", [P, SEQ], F32)
    exact = [sb(f"exact{i}", [P, SEQ], F32) for i in range(2)]
    parts = [sb(f"parts{i}", [P, PARTS, SEQ], BF16) for i in range(2)]
    stack = [[[sb(f"stack{p}{i}{s}", [P, HG, SEQ], BF16) for s in range(2)] for i in range(2)] for p in range(2)]
    values = [sb(f"values{p}", [P, QT, HG * HD], F32) for p in range(2)]
    probs = [sb(f"probs{i}", [P, HG, CHUNK], F32) for i in range(2)]
    maxima = sb("maxima", [P, HG, QT], F32)
    neg_parts = sb("neg_parts", [HG * QT, PARTS, P], BF16)
    neg_rest = sb("neg_rest", [HG * QT, P], F32)
    recip = sb("recip", [P, CHUNK], F32)
    catT = sb("catT", [P, GROUPS, SEQ], F32)
    y = sb("y", [P, QT, D], F32)
    wl = catT[:, 0:2, :].rearrange("p g s -> p (g s)").rearrange("p (h d) -> p h d", h=HEADS)
    w3 = catT[:, 2:4, :].rearrange("p g s -> p (g s)")[:, 0:3 * HEADS * HD]\
        .rearrange("p (j h d) -> p j h d", j=3, h=HEADS)
    bv_wide = y[:, 0:GROUPS, :]
    stats = sb("stats", [P, QT, 6], F32)
    moments = sb("moments", [P, QT, 2], F32)
    rstd = sb("rstd", [P, QT], F32)
    eps = sb("eps", [P, 1], F32)

    passed = sem("passed")
    weights_loaded = sem("weights_loaded")
    consts_loaded = sem("consts_loaded")
    x_next_loaded = sem("x_next_loaded")
    x_here_loaded = sem("x_here_loaded")
    setup_done = sem("setup_done")
    bias_spread = sem("bias_spread")
    copied = sem("copied")
    wide_full = [sem(f"wide_full{i}") for i in range(2)]
    wide_free = [sem(f"wide_free{i}") for i in range(2)]
    rounded = sem("rounded")
    split = sem("split")
    stacked = [[sem(f"stacked{p}{i}") for i in range(2)] for p in range(2)]
    rows_split = sem("rows_split")
    rows_stacked = sem("rows_stacked")
    score_full = sem("score_full")
    exponentials = sem("exponentials")
    mixes = sem("mixes")
    mixed_free = sem("mixed_free")
    recip_ready = sem("recip_ready")
    moments_ready = sem("moments_ready")
    deviation = sem("deviation")
    rstd_ready = sem("rstd_ready")
    centred = sem("centred")
    normed = sem("normed")

    LOADS_W, LOADS_C = 8, 3
    SETUP_OPS = 7
    STACK_INC = 16 * HG * 2 * len(Q_STACK[0])
    ROWS_INC = 16 * PARTS
    uses = {False: iteration_uses(False), True: iteration_uses(True)}
    per_iter = len(uses[False])
    assert per_iter % 2 == 0

    def prologue_use(name):
        n = PROLOGUE_USES.index(name)
        return n % 2, n // 2

    def loop_use(b, g, name, last):
        n = len(PROLOGUE_USES) + uses[last].index((g, name))
        return n % 2, b * (per_iter // 2) + n // 2

    def using(b, g, name, last):
        return prologue_use(name) if b is None else loop_use(b, g, name, last)

    def wait_empty(eng, buf, k):
        eng.wait_ge(wide_free[buf], k)

    def wait_read(eng, buf, k):
        eng.wait_ge(wide_free[buf], k + 1)

    def next_group(b, g):
        return 0 if b is None else GROUPS * b + g + 1

    def stacked_before(b, g, parity):
        if b is None:
            return 0
        return 2 * b + (g + 1 + (1 if parity == 0 else 0)) // 2

    def looped(eng, body):
        with eng.Fori(0, B - 1) as b:
            body(b, False)
        body(B - 1, True)

    block = ctx.enter_context(nc.Block())

    @block.sync
    def _(sp):
        sp.dma_start(wl, ins["Wl"].rearrange("h o i -> o h i")).then_inc(weights_loaded, 16)
        for j, name in enumerate(("Wq", "Wk", "Wv")):
            sp.dma_start(w3[:, j], ins[name].rearrange("h o d -> o h d")).then_inc(weights_loaded, 16)
        sp.dma_start(blT[:], ins["blT"]).then_inc(weights_loaded, 16)
        sp.dma_start(woT[:], ins["WoT"].rearrange("(g p) d -> p g d", p=P)).then_inc(weights_loaded, 16)
        sp.dma_start(bo[:], ins["bo"].rearrange("(a d) -> a d", a=1).broadcast_to([P, D])).then_inc(weights_loaded, 16)
        sp.dma_start(wtok[:], ins["Wtok"]).then_inc(weights_loaded, 16)
        sp.dma_start(cst[:], ins["cst"]).then_inc(consts_loaded, 16)
        sp.dma_start(peT[:], ins["peT"]).then_inc(consts_loaded, 16)
        sp.dma_start(peb[:], ins["pe"].rearrange("(t p) d -> p t d", p=P)).then_inc(consts_loaded, 16)
        sp.dma_start(x_next[:], ins["xT"][0]).then_inc(x_next_loaded, 16)

        def stack_parts(b, g):
            n = next_group(b, g)
            par = (g + 1) % 2 if b is not None else 0
            for s in range(2):
                for i, plan in enumerate((Q_STACK, K_STACK)):
                    for row in sorted(range(len(plan[s])), key=lambda r: plan[s][r]):
                        part = plan[s][row]
                        if part == 0:
                            sp.wait_ge(rounded, 2 * n + i + 1)
                        else:
                            sp.wait_ge(split, 6 * n + ((2, 4), (5, 6))[part - 1][i])
                        for h in range(HG):
                            sp.dma_start(stack[par][i][s][HD * row:HD * row + HD, h, :],
                                         parts[i][HD * h:HD * h + HD, part, :]).then_inc(stacked[par][s], 16)

        def stack_rows(b, g):
            n = next_group(b, g)
            par = (g + 1) % 2 if b is not None else 0
            for part in range(PARTS):
                sp.wait_ge(rows_split, 3 * n + part + 1)
                dst = stack[par][0][0][EXACT + part:EXACT + part + 1, :, :].rearrange("o h (t q) -> o (h t) q", q=P)
                sp.dma_start(dst, neg_parts[:, part, :]).then_inc(rows_stacked, 16)

        stack_parts(None, 0)
        stack_rows(None, 0)

        def body(b, last):
            for g in range(GROUPS):
                if not (last and g == GROUPS - 1):
                    stack_parts(b, g)
                if g == 0:
                    if not last:
                        sp.dma_start(x_next[:], ins["xT"][bass.ds(b + 1, 1)].rearrange("o f s -> (o f) s"))\
                          .then_inc(x_next_loaded, 16)
                    sp.dma_start(x_here[:], ins["xT"][bass.ds(b, 1)].rearrange("o f s -> (o f) s"))\
                      .then_inc(x_here_loaded, 16)
                if not (last and g == GROUPS - 1):
                    stack_rows(b, g)

        looped(sp, body)

    @block.tensor
    def _(pe):
        pe.wait_ge(weights_loaded, 16 * LOADS_W)
        for half in range(2):
            buf, _k = prologue_use(f"fold{half}")
            for hh in range(8):
                h = 8 * half + hh
                for j in range(3):
                    o = wide[buf][:, 512 * (hh // 4) + 96 * (hh % 4) + HD * j:][:, 0:HD]
                    mm = nc.tensor.matmul(o, wl[:, h, :], w3[:, j, h, :], start=True, stop=True)
            mm.then_inc(wide_full[buf], 1)
        buf, k = prologue_use("bias")
        wait_empty(pe, buf, k)
        for j in range(3):
            for h in range(HEADS):
                hh, col = h % HG, j * GROUPS + h // HG
                mm = nc.tensor.matmul(wide[buf][HD * hh:HD * hh + HD, col:col + 1], w3[:, j, h, :],
                                      blT[:, h:h + 1], start=True, stop=True)
        mm.then_inc(wide_full[buf], 1)
        buf, k = prologue_use("outbias")
        wait_empty(pe, buf, k)
        pe.wait_ge(bias_spread, GROUPS)
        for g in range(GROUPS):
            mm = nc.tensor.matmul(wide[buf][:, 0:D], bv_wide[:, g, :], woT[:, g, :],
                                  start=(g == 0), stop=(g == GROUPS - 1))
        mm.then_inc(wide_full[buf], 1)
        pe.wait_ge(setup_done, SETUP_OPS)
        for half in range(2):
            wait_read(pe, *prologue_use(f"fold{half}"))

        def embed(b, g, last):
            buf, k = using(b, g, "embed", last)
            wait_empty(pe, buf, k)
            pe.wait_ge(x_next_loaded, 16 if b is None else 16 * (b + 2))
            for c in range(2):
                mm = nc.tensor.matmul(wide[buf][:, CHUNK * c:CHUNK * (c + 1)], wtok[:],
                                      x_next[:, CHUNK * c:CHUNK * (c + 1)], start=True, stop=True)
            mm.then_inc(wide_full[buf], 1)

        def project(b, g, j, last):
            buf, k = using(b, g, "qkv"[j], last)
            gn = 0 if b is None else (g + 1) % GROUPS
            if j == 0:
                if b is None or g == GROUPS - 1:
                    wait_read(pe, *using(b, g, "embed", last))
            wait_empty(pe, buf, k)
            w = wqkv[:, j, P * gn:P * (gn + 1)]
            if j < 2:
                for c in range(2):
                    mm = nc.tensor.matmul(wide[buf][:, CHUNK * c:CHUNK * (c + 1)], w,
                                          h0T[:, CHUNK * c:CHUNK * (c + 1)], start=True, stop=True)
            else:
                for t in range(QT):
                    mm = nc.tensor.matmul(wide[buf][:, P * t:P * (t + 1)], h0T[:, P * t:P * (t + 1)], w,
                                          start=True, stop=True)
            mm.then_inc(wide_full[buf], 1)

        def max_scores(b, g, piece, last):
            qt, heads = piece
            buf, k = using(b, g, ("max",) + piece, last)
            par = 0 if b is None else (g + 1) % 2
            if piece == PIECES[0]:
                pe.wait_ge(stacked[par][0], STACK_INC * (1 + stacked_before(b, g, par)))
            wait_empty(pe, buf, k)
            qs, ks = stack[par][0][0], stack[par][1][0]
            width = P * (qt + 1)
            for x, h in enumerate(heads):
                at = piece_column(qt, x)
                lhsT = qs[0:EXACT, h, P * qt:P * (qt + 1)]
                for k0 in range(0, width, CHUNK):
                    w = min(CHUNK, width - k0)
                    diagonal = k0 + w == width
                    nc.tensor.matmul(wide[buf][:, at + k0:at + k0 + w], lhsT, ks[0:EXACT, h, k0:k0 + w],
                                     start=True, stop=not diagonal)
                mm = nc.tensor.matmul(wide[buf][:, at + width - P:at + width], ident16, above,
                                      start=False, stop=True)
            mm.then_inc(wide_full[buf], 1)

        def turn_maxima(b, g, last):
            buf, k = using(b, g, "rows", last)
            wait_empty(pe, buf, k)
            wait_read(pe, *using(b, g, ("max",) + PIECES[-2], last))
            wait_read(pe, *using(b, g, ("max",) + PIECES[-1], last))
            nc.tensor.transpose(wide[buf][0:HG * QT, 0:P], maxima[:].rearrange("p h t -> p (h t)"), ident)\
              .then_inc(wide_full[buf], 1)

        def key_scores(b, g, u, h):
            c, kt = UNITS[u]
            q0, w = unit_span(c, kt)
            par, n = g % 2, GROUPS * b + g
            qs, ks = stack[par][0], stack[par][1]
            e = score[h % 2]
            if u == 0 and h == 0:
                pe.wait_ge(rows_stacked, ROWS_INC * (n + 1))
                pe.wait_ge(stacked[par][1], STACK_INC * (2 * b + g // 2 + 1))
            pe.wait_ge(exponentials, 48 * n + HG * u + h + 1)
            diagonal = P * kt >= CHUNK * c
            nc.tensor.matmul(e[:, 0:w], ks[0][0:EXACT + PARTS, h, P * kt:P * (kt + 1)],
                             qs[0][0:EXACT + PARTS, h, q0:q0 + w], start=True, stop=False)
            mm = nc.tensor.matmul(e[:, 0:w], ks[1][0:EXACT, h, P * kt:P * (kt + 1)],
                                  qs[1][0:EXACT, h, q0:q0 + w], start=False, stop=not diagonal)
            if diagonal:
                mm = nc.tensor.matmul(e[:, 0:P], ident16, below, start=False, stop=True)
            mm.then_inc(score_full, 1)

        def mix(b, g, u):
            c, kt = UNITS[u]
            q0, w = unit_span(c, kt)
            off = q0 - CHUNK * c
            n = GROUPS * b + g
            first, final = kt == 0, P * (kt + 1) == CHUNK * (c + 1)
            if first:
                pe.wait_ge(mixed_free, 1 + 2 * n + c)
            pe.wait_ge(exponentials, 2 + 48 * n + HG * (u + 1))
            for h in range(HG):
                rows = slice(HD * h, HD * h + HD)
                nc.tensor.matmul(mixed[rows, off:off + w], values[g % 2][:, kt, rows], probs[u % 2][:, h, 0:w],
                                 start=first, stop=final)
            for h in range(HG):
                rows = slice(HD * h, HD * h + HD)
                mm = nc.tensor.matmul(total[rows, off:off + w], ones[:], probs[u % 2][:, h, 0:w],
                                      start=first, stop=final)
            mm.then_inc(mixes, 1)

        def out_map(b, last):
            buf, k = loop_use(b, GROUPS - 1, "out", last)
            wait_empty(pe, buf, k)
            pe.wait_ge(x_here_loaded, 16 * (b + 1))
            pe.wait_ge(mixed_free, 1 + 2 * GROUPS * (b + 1))
            for t in range(QT):
                cols = slice(P * t, P * (t + 1))
                for g in range(GROUPS):
                    nc.tensor.matmul(wide[buf][:, cols], catT[:, g, cols], woT[:, g, :], start=(g == 0), stop=False)
                mm = nc.tensor.matmul(wide[buf][:, cols], x_here[:, cols], wtok[:], start=False, stop=True)
            mm.then_inc(wide_full[buf], 1)

        embed(None, 0, False)
        for j in range(3):
            project(None, 0, j, False)
        for piece in PIECES:
            max_scores(None, 0, piece, False)
        turn_maxima(None, 0, False)

        def body(b, last):
            for g in range(GROUPS):
                ahead = not (last and g == GROUPS - 1)
                for u in range(len(UNITS)):
                    todo = list(pieces_at(u)) if ahead else []
                    for h in range(HG):
                        key_scores(b, g, u, h)
                        if todo:
                            max_scores(b, g, todo.pop(0), last)
                    if u >= 1:
                        mix(b, g, u - 1)
                    if ahead and u == 0:
                        if g == GROUPS - 1:
                            embed(b, g, last)
                        project(b, g, 0, last)
                        project(b, g, 1, last)
                    if ahead and u == 1:
                        project(b, g, 2, last)
                    if ahead and u == 10:
                        turn_maxima(b, g, last)
                mix(b, g, len(UNITS) - 1)
            out_map(b, last)

        looped(pe, body)

    @block.scalar
    def _(act):
        for half in range(2):
            buf, k = prologue_use(f"fold{half}")
            act.wait_ge(wide_full[buf], k + 1)
            src = wide[buf][:].rearrange("p (a r) -> p a r", a=2)[:, :, 0:384]\
                .rearrange("p a (h j d) -> p a h j d", h=4, j=3)
            for j in range(3):
                for a in range(2):
                    dst = wqkv[:, j, 256 * half + 128 * a:256 * half + 128 * (a + 1)]
                    final = j == 2 and a == 1
                    nc.scalar.copy(dst.rearrange("p (h d) -> p h d", h=4), src[:, a, :, j, :])\
                      .then_inc(wide_free[buf] if final else copied, 1)

        def round_operand(b, g, i, last):
            buf, k = using(b, g, "qk"[i], last)
            n = next_group(b, g)
            gn = 0 if b is None else (g + 1) % GROUPS
            if b is not None:
                before = g % 2
                for s in range(2):
                    act.wait_ge(stacked[before][s], STACK_INC * stacked_before(b, g, before))
            act.wait_ge(wide_full[buf], k + 1)
            bcol = bias[:, i * GROUPS + gn:i * GROUPS + gn + 1]
            nc.scalar.activation(parts[i][:, 0, :], wide[buf][:], ACT.Identity, bias=bcol).then_inc(rounded, 1)
            nc.scalar.activation(exact[i][:], wide[buf][:], ACT.Identity, bias=bcol).then_inc(wide_free[buf], 1)

        def copy_values(b, g, last):
            buf, k = using(b, g, "v", last)
            par = 0 if b is None else (g + 1) % 2
            act.wait_ge(wide_full[buf], k + 1)
            nc.scalar.copy(values[par][:].rearrange("p t c -> p (t c)"), wide[buf][:]).then_inc(wide_free[buf], 1)

        wait_read(act, *prologue_use("bias"))
        for i in range(2):
            round_operand(None, 0, i, False)
        copy_values(None, 0, False)

        def body(b, last):
            for g in range(GROUPS):
                n = GROUPS * b + g
                ahead = not (last and g == GROUPS - 1)
                for u in range(len(UNITS)):
                    _q0, w = unit_span(*UNITS[u])
                    act.wait_ge(mixes, 12 * n + u + 1)
                    for h in range(HG):
                        act.wait_ge(score_full, 48 * n + HG * u + h + 1)
                        nc.scalar.activation(probs[u % 2][:, h, 0:w], score[h % 2][:, 0:w], ACT.Exp)\
                          .then_inc(exponentials, 1)
                    if ahead and u == 1:
                        round_operand(b, g, 0, last)
                        round_operand(b, g, 1, last)
                    if ahead and u == 2:
                        copy_values(b, g, last)
            act.wait_ge(moments_ready, 2 * QT * (b + 1))
            nc.scalar.activation(rstd[:], moments[:, :, 1], ACT.Sqrt, bias=eps[:, 0:1]).then_inc(deviation, 1)

        looped(act, body)

    @block.gpsimd
    def _(pool):
        def split_operands(b, g, last):
            n = next_group(b, g)
            for i in range(2):
                pool.wait_ge(rounded, 2 * n + i + 1)
                wait_read(pool, *using(b, g, "qk"[i], last))
                nc.gpsimd.tensor_tensor(exact[i][:], exact[i][:], parts[i][:, 0, :], ALU.subtract).then_inc(split, 1)
                pool.wait_ge(split, 6 * n + 2 * i + 1)
                pool.sem_inc(passed, 1)
                nc.gpsimd.tensor_copy(parts[i][:, 1, :], exact[i][:]).then_inc(split, 1)
            for i in range(2):
                pool.wait_ge(split, 6 * n + 4)
                nc.gpsimd.tensor_tensor(parts[i][:, 2, :], exact[i][:], parts[i][:, 1, :], ALU.subtract)\
                  .then_inc(split, 1)

        split_operands(None, 0, False)

        def body(b, last):
            for g in range(GROUPS):
                if not (last and g == GROUPS - 1):
                    split_operands(b, g, last)

        looped(pool, body)

    @block.vector
    def _(dve):
        nc.vector.memset(ones[:], 1.0).then_inc(setup_done, 1)
        nc.vector.memset(eps[:], EPS).then_inc(setup_done, 1)
        nc.vector.memset(bv_wide, 0.0).then_inc(setup_done, 1)
        dve.sem_inc(exponentials, 2)
        dve.sem_inc(mixed_free, 1)
        dve.sem_inc(mixes, 2)
        for par in range(2):
            nc.vector.memset(stack[par][1][0][EXACT:EXACT + PARTS, :, :], 1.0).then_inc(setup_done, 1)
        dve.wait_ge(consts_loaded, 16 * LOADS_C)
        nc.vector.tensor_copy(cst16[:], cst[:]).then_inc(setup_done, 1)
        buf, k = prologue_use("bias")
        dve.wait_ge(wide_full[buf], k + 1)
        nc.vector.tensor_copy(bias[:], wide[buf][:, 0:3 * GROUPS]).then_inc(wide_free[buf], 1)
        wait_read(dve, buf, k)
        dve.wait_ge(setup_done, 6)
        for g in range(GROUPS):
            nc.vector.tensor_scalar(bv_wide[:, g, :], bv_wide[:, g, :], bias[:, 2 * GROUPS + g:2 * GROUPS + g + 1],
                                    None, ALU.add).then_inc(bias_spread, 1)
        buf, k = prologue_use("outbias")
        dve.wait_ge(wide_full[buf], k + 1)
        dve.wait_ge(weights_loaded, 16 * LOADS_W)
        nc.vector.tensor_tensor(bo[:], bo[:], wide[buf][:, 0:D], ALU.add).then_inc(wide_free[buf], 1)
        wait_read(dve, buf, k)
        nc.vector.tensor_tensor(peb[:], peb[:], bo[:, None, :].broadcast_to([P, QT, D]), ALU.add)\
          .then_inc(setup_done, 1)
        dve.wait_ge(setup_done, SETUP_OPS)

        def add_positions(b, g, last):
            buf, k = using(b, g, "embed", last)
            dve.wait_ge(wide_full[buf], k + 1)
            nc.vector.tensor_tensor(h0T[:], wide[buf][:], peT[:], ALU.add).then_inc(wide_free[buf], 1)

        def piece_max(b, g, piece, last):
            qt, heads = piece
            buf, k = using(b, g, ("max",) + piece, last)
            width, n = P * (qt + 1), len(heads)
            dve.wait_ge(wide_full[buf], k + 1)
            if n == 4 and qt == 1:
                src = wide[buf][:].rearrange("p (h w) -> p h w", h=4)
            elif n == 4:
                src = wide[buf][:, 0:CHUNK].rearrange("p (h w) -> p h w", h=4)
            elif n == 2:
                src = wide[buf][:].rearrange("p (h w) -> p h w", h=2)[:, :, 0:width]
            else:
                src = wide[buf][:, None, 0:width]
            nc.vector.tensor_reduce(maxima[:, heads[0]:heads[0] + n, qt], src, AX_X, ALU.max)\
              .then_inc(wide_free[buf], 1)

        def split_maxima(b, g, last):
            buf, k = using(b, g, "rows", last)
            n = next_group(b, g)
            src = wide[buf][0:HG * QT, 0:P]
            dve.wait_ge(wide_full[buf], k + 1)
            if b is not None:
                dve.wait_ge(rows_stacked, ROWS_INC * n)
            nc.vector.tensor_scalar(neg_parts[:, 0, :], src, -1.0, None, ALU.mult).then_inc(rows_split, 1)
            dve.wait_ge(rows_split, 3 * n + 1)
            nc.vector.scalar_tensor_tensor(neg_rest[:], src, -1.0, neg_parts[:, 0, :], ALU.mult, ALU.subtract)\
              .then_inc(wide_free[buf], 1)
            wait_read(dve, buf, k)
            nc.vector.tensor_copy(neg_parts[:, 1, :], neg_rest[:]).then_inc(rows_split, 1)
            dve.wait_ge(rows_split, 3 * n + 2)
            nc.vector.tensor_tensor(neg_parts[:, 2, :], neg_rest[:], neg_parts[:, 1, :], ALU.subtract)\
              .then_inc(rows_split, 1)

        def normalise(b, g, c):
            n = GROUPS * b + g
            dve.wait_ge(mixes, 2 + 12 * n + (4, 12)[c])
            nc.vector.reciprocal(recip[:], total[:]).then_inc(recip_ready, 1)
            dve.wait_ge(recip_ready, 2 * n + c + 1)
            nc.vector.tensor_tensor(catT[:, g, CHUNK * c:CHUNK * (c + 1)], mixed[:], recip[:], ALU.mult)\
              .then_inc(mixed_free, 1)

        def layernorm(b, last):
            buf, k = loop_use(b, GROUPS - 1, "out", last)
            dve.wait_ge(wide_full[buf], k + 1)
            nc.vector.tensor_tensor(y[:].rearrange("p t d -> p (t d)"), wide[buf][:],
                                    peb[:].rearrange("p t d -> p (t d)"), ALU.add).then_inc(wide_free[buf], 1)
            wait_read(dve, buf, k)
            for t in range(QT):
                nc.vector.bn_stats(stats[:, t, :], y[:, t, :]).then_inc(moments_ready, 1)
            dve.wait_ge(moments_ready, 2 * QT * b + QT)
            dve.sem_inc(passed, 1)
            for t in range(QT):
                nc.vector.bn_aggr(moments[:, t, :], stats[:, t, :]).then_inc(moments_ready, 1)
            dve.wait_ge(moments_ready, 2 * QT * (b + 1))
            nc.vector.tensor_tensor(y[:], y[:], moments[:, :, 0:1].broadcast_to([P, QT, D]), ALU.subtract)\
              .then_inc(centred, 1)
            dve.wait_ge(deviation, b + 1)
            nc.vector.reciprocal(rstd[:], rstd[:]).then_inc(rstd_ready, 1)
            dve.wait_ge(centred, b + 1)
            dve.wait_ge(rstd_ready, b + 1)
            nc.vector.tensor_tensor(h1[:, bass.ds(b * QT, QT), :], y[:],
                                    rstd[:, :, None].broadcast_to([P, QT, D]), ALU.mult).then_inc(normed, 1)

        add_positions(None, 0, False)
        for piece in PIECES:
            piece_max(None, 0, piece, False)
        split_maxima(None, 0, False)

        def body(b, last):
            for g in range(GROUPS):
                ahead = not (last and g == GROUPS - 1)
                for u in range(len(UNITS)):
                    if ahead:
                        for piece in pieces_at(u):
                            piece_max(b, g, piece, last)
                    if ahead and u == 0 and g == GROUPS - 1:
                        add_positions(b, g, last)
                    if u == 4:
                        normalise(b, g, 0)
                if ahead:
                    split_maxima(b, g, last)
                normalise(b, g, 1)
            layernorm(b, last)
            dve.wait_ge(normed, b + 1)

        looped(dve, body)

    return ctx


def piece_column(qt, x):
    return (P, 2 * P, CHUNK, CHUNK, 0, 0, 0, 0)[qt] * x


TILES = B * SEQ // P
KEYS, TOPK, FH = 64, 8, 8
EXPERTS = KEYS * KEYS
BLOCKS = EXPERTS // P
SLOTS = 2 * FH
CHOSEN = FH * TOPK
CANDS = 20
HALF = P // 2
BANK_TOKENS = CHUNK // BLOCKS
BANKS = P // BANK_TOKENS
SCALE = float(2 ** 14)
FLOOR = 12582912.0


def candidates(a, b, out):
    rows = lambda lo, hi, n: a[:, :, lo:hi, None].broadcast_to([P, FH, hi - lo, n])
    cols = lambda n, m: b[:, :, None, 0:n].broadcast_to([P, FH, m, n])
    at = lambda lo, m, n: out[:, :, lo:lo + m * n].rearrange("p h (m n) -> p h m n", m=m)
    return [(rows(0, 1, 8), cols(8, 1), at(0, 1, 8)), (rows(1, 2, 4), cols(4, 1), at(8, 1, 4)),
            (rows(2, 4, 2), cols(2, 2), at(12, 2, 2)), (rows(4, 8, 1), cols(1, 4), at(16, 4, 1))]


def feed_forward(nc, ins, h1, out, outer):
    ctx = outer.enter_context(ExitStack())

    def sb(name, shape, dt):
        return ctx.enter_context(nc.sbuf_tensor(name, shape, dt))

    def sem(name):
        return ctx.enter_context(nc.semaphore(name))

    def psum(name, shape):
        return ctx.enter_context(nc.psum_tensor(name, shape, F32))

    key_ps = psum("key_ps", [P, SLOTS * KEYS])
    turn_ps = psum("turn_ps", [P, CHUNK])
    inner_ps = psum("inner_ps", [P, 2, CHUNK])
    weight_ps = psum("weight_ps", [P, 2, CHUNK])
    up_ps = psum("up_ps", [P, CHUNK])

    down = sb("down", [P, BLOCKS, P], F32)
    up = sb("up", [P, BLOCKS, D], F32)
    wqT = up[0:KEYS, 0:SLOTS, :]
    keysT = up[0:KEYS, SLOTS:SLOTS + SLOTS // 2, :].rearrange("c a b -> c (a b)")\
        .rearrange("c (s n) -> c s n", s=SLOTS)
    bqT = up[0:KEYS, BLOCKS - 1, 0:SLOTS]
    wkey = sb("wkey", [P, SLOTS * KEYS], F32)
    bkey_row = sb("bkey_row", [1, PARTS, SLOTS * KEYS], BF16)
    bkey_rest = sb("bkey_rest", [1, SLOTS * KEYS], F32)
    bkey = sb("bkey", [P, SLOTS * KEYS], BF16)
    ones16 = sb("ones16", [P, P], BF16)
    cst = sb("cst_ffn", [P, 2, P], F32)
    ident, iota = cst[:, 0, :], cst[:, 1, :]
    numbers = sb("numbers", [P, P, HALF], F16)
    eps = sb("eps_ffn", [P, 1], F32)

    xs = [sb(f"xs{i}", [P, D], F32) for i in range(2)]
    xT = [sb(f"xT{i}", [P, P], F32) for i in range(2)]
    keyscore = sb("keyscore", [P, SLOTS, KEYS], F32)
    tops = sb("tops", [P, FH, 2, TOPK], F32)
    ranks = sb("ranks", [P, FH, 2, TOPK], U32)
    ranksf = sb("ranksf", [P, FH, 2, TOPK], F32)
    cand = sb("cand", [P, FH, CANDS], F32)
    codes = sb("codes", [P, FH, CANDS], F32)
    best = sb("best", [P, FH, TOPK], F32)
    place = sb("place", [P, FH, TOPK], U32)
    placef = sb("placef", [P, FH, TOPK], F32)
    below_max = sb("below_max", [P, FH, TOPK], F32)
    expo = sb("expo", [P, FH, TOPK], F32)
    denom = sb("denom", [P, FH], F32)
    match = sb("match", [P, CANDS, CHOSEN], F32)
    expert = sb("expert", [P, CHOSEN], F32)
    choice = sb("choice", [P, 3, CHOSEN], F32)
    turned16 = sb("turned16", [P, 2, P], F16)
    weight16 = sb("weight16", [P, P], F16)
    row_hot = [sb(f"row_hot{i}", [P, P, HALF], F16) for i in range(2)]
    block_hot = [sb(f"block_hot{i}", [P, BLOCKS, HALF], F16) for i in range(2)]
    vals = sb("vals", [P, BLOCKS, P], F32)
    y = sb("y_ffn", [P, D], F32)
    stats = sb("stats_ffn", [P, 6], F32)
    moments = sb("moments_ffn", [P, 2], F32)
    rstd = sb("rstd_ffn", [P, 1], F32)
    result = [sb(f"result{i}", [P, D], F32) for i in range(2)]

    passed = sem("passed_ffn")
    small_loaded = sem("small_loaded")
    down_loaded = sem("down_loaded")
    up_loaded = sem("up_loaded")
    bias_loaded = sem("bias_loaded")
    ffn_setup = sem("ffn_setup")
    key_folded = sem("key_folded")
    key_copied = sem("key_copied")
    bias_parts = sem("bias_parts")
    x_copied = sem("x_copied")
    x_turned = sem("x_turned")
    xT_ready = sem("xT_ready")
    keys_scored = sem("keys_scored")
    keys_ready = sem("keys_ready")
    topped = sem("topped")
    summed = sem("summed")
    picked = sem("picked")
    coding = sem("coding")
    lowered = sem("lowered")
    matching = sem("matching")
    exponed = sem("exponed")
    deciding = sem("deciding")
    choices_turned = sem("choices_turned")
    turned_ready = sem("turned_ready")
    low_ready = sem("low_ready")
    built = sem("built")
    inner_full = sem("inner_full")
    rectified = sem("rectified")
    weight_full = sem("weight_full")
    weighted = sem("weighted")
    up_full = sem("up_full")
    added = sem("added")
    moments_done = sem("moments_done")
    deviated = sem("deviated")
    inverted = sem("inverted")
    finished = sem("finished")
    stored = [sem(f"stored{i}") for i in range(2)]
    DECIDE = 7

    def looped(eng, body):
        with eng.Fori(0, TILES // 2 - 1) as pair:
            for par in range(2):
                body(2 * pair + par, pair, par, 2)
        body(TILES - 2, TILES // 2 - 1, 0, 1)
        body(TILES - 1, TILES // 2 - 1, 1, 0)

    block = ctx.enter_context(nc.Block())

    @block.sync
    def _(sp):
        sp.dma_start(wqT, ins["WqT_ffn"]).then_inc(small_loaded, 16)
        sp.dma_start(keysT, ins["keysT"]).then_inc(small_loaded, 16)
        sp.dma_start(bqT, ins["bqT"]).then_inc(small_loaded, 16)
        sp.dma_start(cst[:], ins["cst_ffn"]).then_inc(small_loaded, 16)
        sp.dma_start(down[:], ins["downT"].rearrange("d (n e) -> d n e", e=P)).then_inc(down_loaded, 16)
        sp.wait_ge(bias_parts, 4)
        for part in range(PARTS):
            sp.dma_start(bkey[part:part + 1, :], bkey_row[:, part, :]).then_inc(bias_loaded, 16)
        sp.wait_ge(key_folded, 2)
        sp.dma_start(up[:], ins["up"].rearrange("(n e) d -> e n d", e=P)).then_inc(up_loaded, 16)

        def body(i, pair, par, ahead):
            sp.wait_ge(finished, i + 1)
            dst = out[bass.ds(i, 1)] if not isinstance(i, int) else out[i:i + 1]
            sp.dma_start(dst.rearrange("o p d -> (o p) d"), result[par][:]).then_inc(stored[par], 16)

        looped(sp, body)
        for par in range(2):
            sp.wait_ge(stored[par], 16 * (TILES // 2 + 1))

    @block.tensor
    def _(pe):
        pe.wait_ge(small_loaded, 16 * 4)
        for s in range(SLOTS):
            mm = nc.tensor.matmul(key_ps[:, KEYS * s:KEYS * (s + 1)], wqT[:, s, :], keysT[:, s, :],
                                  start=True, stop=True)
        mm.then_inc(key_folded, 1)
        flat = weight_ps[:].rearrange("p a b -> p (a b)")
        for s in range(SLOTS):
            mm = nc.tensor.matmul(flat[0:1, KEYS * s:KEYS * (s + 1)], bqT[:, s:s + 1], keysT[:, s, :],
                                  start=True, stop=True)
        mm.then_inc(key_folded, 1)
        pe.wait_ge(key_copied, 1)
        pe.wait_ge(ffn_setup, 5)
        pe.wait_ge(bias_loaded, 16 * PARTS)

        def turn_tokens(j, par):
            pe.wait_ge(x_copied, j + 1)
            pe.wait_ge(keys_ready, j)
            nc.tensor.transpose(key_ps[:, 0:P], xs[par][:], ident).then_inc(x_turned, 1)

        def score_keys(j, par):
            pe.wait_ge(xT_ready, j + 1)
            for c in range(2):
                cols = slice(CHUNK * c, CHUNK * (c + 1))
                nc.tensor.matmul(key_ps[:, cols], xT[par][:], wkey[:, cols], start=True, stop=False)
                mm = nc.tensor.matmul(key_ps[:, cols], ones16[:], bkey[:, cols], start=False, stop=True)
            mm.then_inc(keys_scored, 1)

        def turn_choices(j):
            pe.wait_ge(deciding, DECIDE * (j + 1))
            pe.wait_ge(low_ready, j)
            for k in range(3):
                for twice in range(2):
                    mm = nc.tensor.matmul(turn_ps[CHOSEN * twice:CHOSEN * (twice + 1), P * k:P * (k + 1)],
                                          choice[:, k, :], ident, start=True, stop=True)
            mm.then_inc(choices_turned, 1)

        def inner(i, par):
            for k in range(BANKS):
                pe.wait_ge(rectified, BANKS * i + k + 1)
                for n in range(4 * k, 4 * k + 4):
                    mm = nc.tensor.matmul(inner_ps[:, k % 2, P * (n % 4):P * (n % 4 + 1)], down[:, n, :], xT[par][:],
                                          start=True, stop=True)
                mm.then_inc(inner_full, 1)

        def expert_weights(i):
            for k in range(BANKS):
                half = k // (BANKS // 2)
                if k % (BANKS // 2) == 0:
                    pe.wait_ge(built, 6 * i + 3 * (half + 1))
                pe.wait_ge(weighted, BANKS * i + k + 1)
                for s in range(BANK_TOKENS):
                    t = BANK_TOKENS * k + s - HALF * half
                    mm = nc.tensor.matmul(weight_ps[:, k % 2, BLOCKS * s:BLOCKS * (s + 1)],
                                          row_hot[half][:, :, t], block_hot[half][:, :, t], start=True, stop=True)
                mm.then_inc(weight_full, 1)

        def up_product(i):
            pe.wait_ge(weighted, 2 + BANKS * (i + 1))
            pe.wait_ge(added, i + 1)
            for n in range(BLOCKS):
                mm = nc.tensor.matmul(up_ps[:, 0:D], vals[:, n, :], up[:, n, :],
                                      start=(n == 0), stop=(n == BLOCKS - 1))
            mm.then_inc(up_full, 1)

        turn_tokens(0, 0)
        score_keys(0, 0)
        turn_choices(0)
        turn_tokens(1, 1)
        score_keys(1, 1)
        pe.wait_ge(down_loaded, 16)
        pe.wait_ge(up_loaded, 16)

        def body(i, pair, par, ahead):
            inner(i, par)
            if ahead == 2:
                turn_tokens(i + 2, par)
                score_keys(i + 2, par)
            if ahead:
                turn_choices(i + 1)
            expert_weights(i)
            up_product(i)

        looped(pe, body)

    @block.scalar
    def _(act):
        act.wait_ge(key_folded, 1)
        nc.scalar.copy(wkey[:], key_ps[:]).then_inc(key_copied, 1)

        def copy_tokens(j, par):
            act.wait_ge(x_turned, j + 1)
            nc.scalar.copy(xT[par][:], key_ps[:, 0:P]).then_inc(xT_ready, 1)

        def copy_keys(j):
            act.wait_ge(topped, 2 * j)
            act.wait_ge(keys_scored, j + 1)
            nc.scalar.copy(keyscore[:].rearrange("p s n -> p (s n)"), key_ps[:]).then_inc(keys_ready, 1)

        def exponentiate(j):
            act.wait_ge(lowered, j + 1)
            act.wait_ge(deciding, DECIDE * j)
            nc.scalar.activation(expo[:], below_max[:], ACT.Exp).then_inc(exponed, 1)

        def copy_choices(j):
            act.wait_ge(built, 6 * j)
            act.wait_ge(choices_turned, j + 1)
            nc.scalar.copy(turned16[:].rearrange("p a t -> p (a t)"), turn_ps[:, 0:2 * P]).then_inc(turned_ready, 1)
            nc.scalar.copy(weight16[:], turn_ps[:, 2 * P:3 * P]).then_inc(turned_ready, 1)

        def rectify(i):
            for k in range(BANKS):
                act.wait_ge(inner_full, BANKS * i + k + 1)
                nc.scalar.activation(vals[:, 4 * k:4 * k + 4, :].rearrange("p n t -> p (n t)"), inner_ps[:, k % 2, :],
                                     ACT.Relu, scale=1.0 / SCALE).then_inc(rectified, 1)

        def deviate(i):
            act.wait_ge(moments_done, 2 * (i + 1))
            nc.scalar.activation(rstd[:], moments[:, 1:2], ACT.Sqrt, bias=eps[:, 0:1]).then_inc(deviated, 1)

        copy_tokens(0, 0)
        copy_keys(0)
        exponentiate(0)
        copy_choices(0)
        copy_tokens(1, 1)
        copy_keys(1)
        exponentiate(1)

        def body(i, pair, par, ahead):
            rectify(i)
            if ahead == 2:
                copy_tokens(i + 2, par)
                copy_keys(i + 2)
            if ahead:
                copy_choices(i + 1)
            if ahead == 2:
                exponentiate(i + 2)
            deviate(i)

        looped(act, body)

    @block.gpsimd
    def _(pool):
        def copy_x(j, par, late):
            if late:
                pool.wait_ge(x_turned, j - 1)
                pool.sem_inc(passed, 1)
            src = h1[:, bass.ds(j, 1), :] if not isinstance(j, int) else h1[:, j:j + 1, :]
            nc.gpsimd.tensor_copy(xs[par][:, None, :], src).then_inc(x_copied, 1)

        def decode(j):
            pool.wait_ge(topped, 2 * (j + 1))
            pool.sem_inc(passed, 1)
            nc.gpsimd.tensor_copy(ranksf[:], ranks[:]).then_inc(coding, 1)
            pool.wait_ge(coding, 3 * j + 1)
            pool.sem_inc(passed, 1)
            nc.gpsimd.tensor_scalar(ranksf[:, :, 0, :], ranksf[:, :, 0, :], float(KEYS), None, ALU.mult)\
              .then_inc(coding, 1)
            pool.wait_ge(coding, 3 * j + 2)
            ops = candidates(ranksf[:, :, 0, :], ranksf[:, :, 1, :], codes)
            for a, b, o in ops:
                last = nc.gpsimd.tensor_tensor(o, a, b, ALU.add)
            last.then_inc(coding, 1)
            pool.wait_ge(picked, 2 * (j + 1))
            pool.wait_ge(exponed, j)
            nc.gpsimd.tensor_tensor(below_max[:], best[:], best[:, :, 0:1].broadcast_to([P, FH, TOPK]),
                                    ALU.subtract).then_inc(lowered, 1)
            nc.gpsimd.tensor_copy(placef[:], place[:]).then_inc(matching, 1)
            pool.wait_ge(matching, 3 * j + 1)
            pool.wait_ge(deciding, DECIDE * j)
            pool.sem_inc(passed, 1)
            flat = placef[:].rearrange("p h k -> p (h k)")
            for c in range(CANDS):
                last = nc.gpsimd.tensor_scalar(match[:, c, :], flat, float(c), None, ALU.is_equal)
            last.then_inc(matching, 1)
            pool.wait_ge(matching, 3 * j + 2)
            pool.wait_ge(coding, 3 * j + 3)
            view = match[:].rearrange("p c (h k) -> p c h k", h=FH)
            per_cand = codes[:].rearrange("p h c -> p c h")[:, :, :, None].broadcast_to([P, CANDS, FH, TOPK])
            nc.gpsimd.tensor_tensor(view, view, per_cand, ALU.mult).then_inc(matching, 1)

        copy_x(0, 0, False)
        copy_x(1, 1, False)
        pool.wait_ge(ffn_setup, 5)
        decode(0)
        decode(1)

        def body(i, pair, par, ahead):
            if ahead == 2:
                copy_x(i + 2, par, True)
                decode(i + 2)

        looped(pool, body)

    @block.vector
    def _(dve):
        dve.sem_inc(rectified, 2)
        dve.sem_inc(weighted, 2)
        dve.sem_inc(added, 1)
        for par in range(2):
            dve.sem_inc(stored[par], 16)
        nc.vector.memset(ones16[:], 1.0).then_inc(ffn_setup, 1)
        nc.vector.memset(eps[:], EPS).then_inc(ffn_setup, 1)
        nc.vector.memset(bkey[:], 0.0).then_inc(ffn_setup, 1)
        dve.wait_ge(ffn_setup, 3)
        dve.wait_ge(small_loaded, 16 * 4)
        nc.vector.tensor_copy(numbers[:], iota[:, :, None].broadcast_to([P, P, HALF])).then_inc(ffn_setup, 1)
        dve.wait_ge(key_folded, 2)
        src = weight_ps[0:1, :, :].rearrange("p a b -> p (a b)")
        nc.vector.tensor_copy(bkey_row[:, 0, :], src).then_inc(bias_parts, 1)
        dve.wait_ge(bias_parts, 1)
        nc.vector.tensor_tensor(bkey_rest[:], src, bkey_row[:, 0, :], ALU.subtract).then_inc(bias_parts, 1)
        dve.wait_ge(bias_parts, 2)
        nc.vector.tensor_copy(bkey_row[:, 1, :], bkey_rest[:]).then_inc(bias_parts, 1)
        dve.wait_ge(bias_parts, 3)
        nc.vector.tensor_tensor(bkey_row[:, 2, :], bkey_rest[:], bkey_row[:, 1, :], ALU.subtract)\
          .then_inc(bias_parts, 1)
        dve.wait_ge(bias_parts, 4)
        nc.vector.memset(denom[:], 0.0).then_inc(ffn_setup, 1)
        dve.wait_ge(ffn_setup, 5)

        def search(j):
            dve.wait_ge(keys_ready, j + 1)
            dve.wait_ge(matching, 3 * j)
            dve.sem_inc(passed, 1)
            for s in range(SLOTS):
                last = nc.vector.max(tops[:, s // 2, s % 2, :], keyscore[:, s, :])
            last.then_inc(topped, 1)
            dve.wait_ge(topped, 2 * j + 1)
            dve.sem_inc(passed, 1)
            for s in range(SLOTS):
                last = nc.vector.max_index(ranks[:, s // 2, s % 2, :], tops[:, s // 2, s % 2, :], keyscore[:, s, :])
            last.then_inc(topped, 1)
            for a, b, o in candidates(tops[:, :, 0, :], tops[:, :, 1, :], cand):
                last = nc.vector.tensor_tensor(o, a, b, ALU.add)
            last.then_inc(summed, 1)
            dve.wait_ge(summed, j + 1)
            dve.sem_inc(passed, 1)
            for h in range(FH):
                last = nc.vector.max(best[:, h, :], cand[:, h, :])
            last.then_inc(picked, 1)
            dve.wait_ge(picked, 2 * j + 1)
            dve.sem_inc(passed, 1)
            for h in range(FH):
                last = nc.vector.max_index(place[:, h, :], best[:, h, :], cand[:, h, :])
            last.then_inc(picked, 1)

        def decide(j):
            n = DECIDE * j
            dve.wait_ge(matching, 3 * (j + 1))
            dve.wait_ge(choices_turned, j)
            nc.vector.tensor_reduce(expert[:], match[:].rearrange("p c x -> p x c"), AX_X, ALU.add)\
              .then_inc(deciding, 1)
            dve.wait_ge(exponed, j + 1)
            nc.vector.tensor_reduce(denom[:], expo[:], AX_X, ALU.add).then_inc(deciding, 1)
            dve.wait_ge(deciding, n + 1)
            nc.vector.tensor_scalar(choice[:, 1, :], expert[:], 1.0 / P, 0.5 - 0.5 / P, ALU.mult, ALU.subtract)\
              .then_inc(deciding, 1)
            dve.wait_ge(deciding, n + 2)
            nc.vector.reciprocal(denom[:], denom[:]).then_inc(deciding, 1)
            dve.wait_ge(deciding, n + 3)
            nc.vector.tensor_scalar(choice[:, 1, :], choice[:, 1, :], FLOOR, FLOOR, ALU.add, ALU.subtract)\
              .then_inc(deciding, 1)
            dve.wait_ge(deciding, n + 4)
            nc.vector.scalar_tensor_tensor(choice[:, 2, :].rearrange("p (h k) -> p h k", h=FH), expo[:], SCALE,
                                           denom[:, :, None].broadcast_to([P, FH, TOPK]), ALU.mult, ALU.mult)\
              .then_inc(deciding, 1)
            dve.wait_ge(deciding, n + 5)
            nc.vector.scalar_tensor_tensor(choice[:, 0, :], choice[:, 1, :], -float(P), expert[:], ALU.mult, ALU.add)\
              .then_inc(deciding, 1)

        def low_parts(j):
            dve.wait_ge(turned_ready, 2 * (j + 1))
            low = weight16[CHOSEN:P, :]
            nc.vector.tensor_tensor(low, turn_ps[CHOSEN:P, 2 * P:3 * P], low, ALU.subtract).then_inc(low_ready, 1)
            dve.wait_ge(low_ready, j + 1)

        def build(j, late):
            for half in range(2):
                cols = slice(HALF * half, HALF * (half + 1))
                if late:
                    dve.wait_ge(weight_full, BANKS * (j - 1) + (BANKS // 2) * (half + 1))

                def over(n, src):
                    return src[:, None, cols].broadcast_to([P, n, HALF])

                nc.vector.tensor_tensor(block_hot[half][:], numbers[:, 0:BLOCKS, :], over(BLOCKS, turned16[:, 1, :]),
                                        ALU.is_equal).then_inc(built, 1)
                nc.vector.tensor_tensor(row_hot[half][:], numbers[:], over(P, turned16[:, 0, :]),
                                        ALU.is_equal).then_inc(built, 1)
                dve.wait_ge(built, 6 * j + 3 * half + 1)
                nc.vector.tensor_tensor(block_hot[half][:], block_hot[half][:], over(BLOCKS, weight16),
                                        ALU.mult).then_inc(built, 1)

        def weigh(i):
            dve.wait_ge(rectified, 2 + BANKS * (i + 1))
            for k in range(BANKS):
                v = vals[:, :, BANK_TOKENS * k:BANK_TOKENS * (k + 1)]
                dve.wait_ge(weight_full, BANKS * i + k + 1)
                nc.vector.tensor_tensor(v, weight_ps[:, k % 2, :].rearrange("p (t n) -> p n t", n=BLOCKS), v,
                                        ALU.mult).then_inc(weighted, 1)

        def moments_of(i):
            dve.wait_ge(up_full, i + 1)
            here = h1[:, bass.ds(i, 1), :] if not isinstance(i, int) else h1[:, i:i + 1, :]
            nc.vector.tensor_tensor(y[:, None, :], up_ps[:, None, 0:D], here, ALU.add).then_inc(added, 1)
            dve.wait_ge(added, i + 2)
            nc.vector.bn_stats(stats[:], y[:]).then_inc(moments_done, 1)
            dve.wait_ge(moments_done, 2 * i + 1)
            dve.sem_inc(passed, 1)
            nc.vector.bn_aggr(moments[:], stats[:]).then_inc(moments_done, 1)

        def finish(i, pair, par):
            dve.wait_ge(deviated, i + 1)
            nc.vector.reciprocal(rstd[:], rstd[:]).then_inc(inverted, 1)
            dve.wait_ge(inverted, i + 1)
            dve.wait_ge(stored[par], 16 * (pair + 1))
            nc.vector.tensor_scalar(result[par][:], y[:], moments[:, 0:1], rstd[:, 0:1], ALU.subtract, ALU.mult)\
              .then_inc(finished, 1)
            dve.wait_ge(finished, i + 1)

        search(0)
        decide(0)
        search(1)
        low_parts(0)
        build(0, False)

        def body(i, pair, par, ahead):
            if ahead:
                decide(i + 1)
            weigh(i)
            if ahead == 2:
                search(i + 2)
            moments_of(i)
            if ahead:
                low_parts(i + 1)
                build(i + 1, True)
            finish(i, pair, par)

        looped(dve, body)

    return ctx


def positions():
    position = np.arange(SEQ * 2, dtype=np.float32)[:, None]
    div_term = np.exp(np.arange(0, D, 2, dtype=np.float32) * (-np.log(10000.0) / D)).astype(np.float32)
    pe = np.zeros((SEQ * 2, D), dtype=np.float32)
    pe[:, 0::2] = np.sin(position * div_term)
    pe[:, 1::2] = np.cos(position * div_term)
    return pe[:SEQ]


FFN_INS = ["WqT_ffn", "keysT", "bqT", "cst_ffn", "downT", "up"]
ATT_INS = ["xT", "Wtok", "Wl", "blT", "Wq", "Wk", "Wv", "WoT", "bo", "pe", "peT", "cst"]


def host_arrays(**a):
    def lay(x):
        return np.ascontiguousarray(x)
    above = np.triu(np.full((P, P), -1e30, np.float32), 1)
    pe = positions()
    return {
        "xT": lay(np.asarray(a["x"]).reshape(B, SEQ, FEAT).transpose(0, 2, 1)),
        "Wtok": lay(a["L0_tok_W"]),
        "Wl": lay(a["L0_attn_Wl"]),
        "blT": lay(np.asarray(a["L0_attn_bl"]).T),
        "Wq": lay(a["L0_attn_Wq"]), "Wk": lay(a["L0_attn_Wk"]), "Wv": lay(a["L0_attn_Wv"]),
        "WoT": lay(np.asarray(a["L0_attn_Wo"]).T),
        "bo": lay(a["L0_attn_bo"]),
        "pe": pe, "peT": lay(pe.T),
        "WqT_ffn": lay(np.asarray(a["L0_ffn_Wq"]).reshape(D, SLOTS, KEYS).transpose(2, 1, 0)),
        "keysT": lay(np.asarray(a["L0_ffn_keys"]).reshape(SLOTS, KEYS, KEYS).transpose(2, 0, 1)),
        "bqT": lay(np.asarray(a["L0_ffn_bq"]).reshape(SLOTS, KEYS).T),
        "cst_ffn": lay(np.stack([np.eye(P, dtype=np.float32), np.tile(np.arange(P, dtype=np.float32), (P, 1))], 1)),
        "downT": lay(np.asarray(a["L0_ffn_w_down"]).T),
        "up": lay(a["L0_ffn_w_up"]),
        "cst": lay(np.stack([np.eye(P, dtype=np.float32), above, above.T], 1)),
    }


def vit_layer(nc, ins, out):
    with ExitStack() as ctx:
        h1 = ctx.enter_context(nc.sbuf_tensor("h1", [P, TILES, D], F32))
        with ExitStack() as first:
            attention(nc, ins, h1, first)
        with ExitStack() as second:
            feed_forward(nc, ins, h1, out, second)


def kernel(**inputs):
    import numpy as _np
    import concourse.bacc as _bacc
    from concourse import mybir as _mybir
    from concourse.bass_utils import run_bass_kernel_spmd as _run

    nc = _bacc.Bacc("TRN2", target_bir_lowering=False, num_devices=1)
    arrays, ins = {}, {}
    for name, a in host_arrays(**inputs).items():
        arrays[f"in_{name}_dram"] = a
        ins[name] = nc.dram_tensor(f"in_{name}_dram", a.shape, _mybir.dt.from_np(a.dtype), kind="ExternalInput").ap()
    out = nc.dram_tensor("out_dram", (TILES, P, D), _mybir.dt.float32, kind="ExternalOutput").ap()
    vit_layer(nc, ins, out)
    r = _run(nc, [arrays], core_ids=[0])
    return _np.asarray(r.results[0]["out_dram"]).reshape(B, SEQ, D)
```

```python
from contextlib import ExitStack

import concourse.bass as bass
import numpy as np
from concourse import mybir
from concourse.alu_op_type import AluOpType as ALU

F32 = mybir.dt.float32
BF16 = mybir.dt.bfloat16
F16 = mybir.dt.float16
I32 = mybir.dt.int32
U32 = mybir.dt.uint32
ACT = mybir.ActivationFunctionType
AX_X = mybir.AxisListType.X

P = 128
B, SEQ, FEAT, D = 8, 1024, 29, 128
HEADS, HD = 16, 32
HG = 4
GROUPS = HEADS // HG
QT = SEQ // P
POOL_HEADS = 3
CHUNK = 512
EPS = 1e-5
PARTS = 2
EXACT = 3 * HD
MAX_UNIT = 64.0

Q_STACK = (0, 1, 0)
K_STACK = (0, 0, 1)
RING = 4

UNITS = [(c, kt) for c in range(SEQ // CHUNK) for kt in range((c + 1) * CHUNK // P)]
PIECES = [(qt, tuple(range(h, h + n))) for qt in range(QT)
          for n in ((4, 4, 2, 2, 1, 1, 1, 1)[qt],) for h in range(0, HG, n)]
PIECE_SLOTS = {4: 4, 5: 4, 6: 4, 7: 4, 8: 4, 9: 2}


TOTAL1_AT = 2
VALUES_AT = 1
PROJECT_AT = 8
ROWS_AT = 9
TOTAL0_AT = 10


def pieces_at(u):
    first = sum(n for v, n in PIECE_SLOTS.items() if v < u)
    return PIECES[first:first + PIECE_SLOTS.get(u, 0)]


def unit_span(c, kt):
    q0 = max(CHUNK * c, P * kt)
    return q0, CHUNK * (c + 1) - q0


PROLOGUE_USES = (["fold0", "fold1", "bias", "outbias", "embed", "q", "k", "v"] + [("max",) + p for p in PIECES]
                 + ["rows", "q1", "k1"])


def iteration_uses(last):
    uses = []
    for g in range(GROUPS):
        one, two = not (last and g >= GROUPS - 1), not (last and g >= GROUPS - 2)
        for u in range(len(UNITS)):
            uses += [(g, ("max",) + p) for p in (pieces_at(u) if one else ())]
            if u == VALUES_AT and one:
                uses.append((g, "v"))
            if u == TOTAL1_AT and g > 0:
                uses.append((g - 1, "total1"))
            if u == PROJECT_AT and two:
                uses += [(g, "embed")] * (g == GROUPS - 2) + [(g, "q"), (g, "k")]
            if u == ROWS_AT and one:
                uses.append((g, "rows"))
            if u == TOTAL0_AT:
                uses.append((g, "total0"))
    return uses + [(GROUPS - 1, "total1"), (GROUPS - 1, "out")]


def attention(nc, ins, h1, outer):
    ctx = outer.enter_context(ExitStack())

    def sb(name, shape, dt):
        return ctx.enter_context(nc.sbuf_tensor(name, shape, dt))

    def sem(name):
        return ctx.enter_context(nc.semaphore(name))

    wide = [ctx.enter_context(nc.psum_tensor(f"wide{i}", [P, SEQ], F32)) for i in range(2)]
    score = [ctx.enter_context(nc.psum_tensor(f"score{i}", [P, CHUNK], F32)) for i in range(2)]
    mixed = [ctx.enter_context(nc.psum_tensor(f"mixed{c}", [P, CHUNK], F32)) for c in range(2)]

    blT = sb("blT", [P, HEADS], F32)
    wqkv = sb("wqkv", [P, 3, HEADS * HD], F32)
    woT = sb("woT", [P, GROUPS, D], F32)
    bo = sb("bo", [P, D], F32)
    bias = sb("bias", [P, 3 * GROUPS], F32)
    wtok = sb("wtok", [FEAT, D], F32)
    cst = sb("cst", [P, 3, P], F32)
    ident = cst[:, 0, :]
    cst16 = sb("cst16", [P, 3, P], BF16)
    ident16, above, below = cst16[:, 0, :], cst16[:, 1, :], cst16[:, 2, :]
    ones = sb("ones", [P, HD], F32)
    peT = sb("peT", [P, SEQ], F32)
    peb = sb("peb", [P, QT, D], F32)

    x_next = sb("x_next", [FEAT, SEQ], F32)
    x_here = sb("x_here", [FEAT, SEQ], F32)
    h0T = sb("h0T", [P, SEQ], F32)
    parts = [sb(f"parts{i}", [P, PARTS, SEQ], F16) for i in range(2)]
    stack = [[sb(f"stack{p}{i}", [P, HG, SEQ], F16) for i in range(2)] for p in range(2)]
    values = [sb(f"values{p}", [P, QT, HG * HD], F32) for p in range(2)]
    probs = [sb(f"probs{i}", [P, HG, CHUNK], F32) for i in range(RING)]
    sums = [sb(f"sums{c}", [P, HG, CHUNK], F32) for c in range(2)]
    maxima = sb("maxima", [P, HG, QT], F32)
    neg_parts = sb("neg_parts", [HG * QT, PARTS, P], F16)
    recip = sb("recip", [P, CHUNK], F32)
    catT = sb("catT", [P, GROUPS, SEQ], F32)
    y = sb("y", [P, QT, D], F32)
    wl = catT[:, 0:2, :].rearrange("p g s -> p (g s)").rearrange("p (h d) -> p h d", h=HEADS)
    w3 = catT[:, 2:4, :].rearrange("p g s -> p (g s)")[:, 0:3 * HEADS * HD]\
        .rearrange("p (j h d) -> p j h d", j=3, h=HEADS)
    bv_wide = y[:, 0:GROUPS, :]
    stats = sb("stats", [P, QT, 6], F32)
    moments = sb("moments", [P, QT, 2], F32)
    rstd = sb("rstd", [P, QT], F32)
    eps = sb("eps", [P, 1], F32)

    passed = sem("passed")
    weights_loaded = sem("weights_loaded")
    consts_loaded = sem("consts_loaded")
    x_next_loaded = sem("x_next_loaded")
    x_here_loaded = sem("x_here_loaded")
    setup_done = sem("setup_done")
    bias_spread = sem("bias_spread")
    copied = sem("copied")
    wide_full = [sem(f"wide_full{i}") for i in range(2)]
    wide_free = [sem(f"wide_free{i}") for i in range(2)]
    rounded = sem("rounded")
    stacked = [sem(f"stacked{p}") for p in range(2)]
    rows_split = sem("rows_split")
    rows_stacked = sem("rows_stacked")
    score_full = sem("score_full")
    exponentials = sem("exponentials")
    mixes = sem("mixes")
    pool_sums = sem("pool_sums")
    dve_sums = sem("dve_sums")
    mixed_free = [sem(f"mixed_free{c}") for c in range(2)]
    moments_ready = sem("moments_ready")
    deviation = sem("deviation")
    rstd_ready = sem("rstd_ready")
    centred = sem("centred")
    normed = sem("normed")

    LOADS_W, LOADS_C = 8, 3
    SETUP_OPS = 7
    STACK_INC = 16 * HG * 2 * len(Q_STACK)
    ROWS_INC = 16 * PARTS
    uses = {False: iteration_uses(False), True: iteration_uses(True)}
    per_iter = len(uses[False])
    assert per_iter % 2 == 0

    def prologue_use(name):
        n = PROLOGUE_USES.index(name)
        return n % 2, n // 2

    def loop_use(b, g, name, last):
        n = len(PROLOGUE_USES) + uses[last].index((g, name))
        return n % 2, b * (per_iter // 2) + n // 2

    def using(b, g, name, last):
        return prologue_use(name) if b is None else loop_use(b, g, name, last)

    def wait_empty(eng, buf, k):
        eng.wait_ge(wide_free[buf], k)

    def wait_read(eng, buf, k):
        eng.wait_ge(wide_free[buf], k + 1)

    def operand(b, g, i):
        return "qk"[i] + ("1" if b is None and g == 1 else "")

    def ahead_of(b, g, step):
        if b is None:
            return g, g, g
        return GROUPS * b + g + step, (g + step) % GROUPS, (g + step) % 2

    def same_parity_before(b, g, step):
        return 0 if b is None else 2 * b + (g + step) // 2

    def add_up(eng, unit_engine, sem_done, b, g, u, h0, h1_):
        c, kt = UNITS[u]
        q0, w = unit_span(c, kt)
        n = GROUPS * b + g
        at = q0 - CHUNK * c
        src = probs[u % RING][:, h0:h1_, 0:w]
        dst = sums[c][:, h0:h1_, at:CHUNK]
        if kt == 0:
            return
        eng.wait_ge(exponentials, 2 + 48 * n + HG * u + h1_)
        if kt == 1:
            eng.wait_ge(mixed_free[c], n + 1)
            before = probs[(u - 1) % RING][:, h0:h1_, :]
            if at:
                eng.sem_inc(passed, 1)
                unit_engine.tensor_scalar(sums[c][:, h0:h1_, 0:at], before[:, :, 0:at], 1.0, None, ALU.mult)
            unit_engine.tensor_tensor(dst, before[:, :, at:CHUNK], src, ALU.add).then_inc(sem_done, 2)
        else:
            eng.wait_ge(sem_done, RING + 12 * n + u)
            unit_engine.tensor_tensor(dst, dst, src, ALU.add).then_inc(sem_done, 1)

    def looped(eng, body):
        with eng.Fori(0, B - 1) as b:
            body(b, False)
        body(B - 1, True)

    block = ctx.enter_context(nc.Block())

    @block.sync
    def _(sp):
        sp.dma_start(wl, ins["Wl"].rearrange("h o i -> o h i")).then_inc(weights_loaded, 16)
        for j, name in enumerate(("Wq", "Wk", "Wv")):
            sp.dma_start(w3[:, j], ins[name].rearrange("h o d -> o h d")).then_inc(weights_loaded, 16)
        sp.dma_start(blT[:], ins["blT"]).then_inc(weights_loaded, 16)
        sp.dma_start(woT[:], ins["WoT"].rearrange("(g p) d -> p g d", p=P)).then_inc(weights_loaded, 16)
        sp.dma_start(bo[:], ins["bo"].rearrange("(a d) -> a d", a=1).broadcast_to([P, D])).then_inc(weights_loaded, 16)
        sp.dma_start(wtok[:], ins["Wtok"]).then_inc(weights_loaded, 16)
        sp.dma_start(cst[:], ins["cst"]).then_inc(consts_loaded, 16)
        sp.dma_start(peT[:], ins["peT"]).then_inc(consts_loaded, 16)
        sp.dma_start(peb[:], ins["pe"].rearrange("(t p) d -> p t d", p=P)).then_inc(consts_loaded, 16)
        sp.dma_start(x_next[:], ins["xT"][0]).then_inc(x_next_loaded, 16)

        def stack_parts(b, g, last):
            n, _gm, par = ahead_of(b, g, 2)
            if b is not None:
                sp.wait_ge(score_full, 48 * (GROUPS * b + g + 1))
            for part in range(PARTS):
                for i, plan in enumerate((Q_STACK, K_STACK)):
                    if part == 0:
                        sp.wait_ge(rounded, 2 * n + i + 1)
                    else:
                        wait_read(sp, *using(b, g, operand(b, g, i), last))
                    for row in [r for r in range(len(plan)) if plan[r] == part]:
                        for h in range(HG):
                            sp.dma_start(stack[par][i][HD * row:HD * row + HD, h, :],
                                         parts[i][HD * h:HD * h + HD, part, :]).then_inc(stacked[par], 16)

        def stack_rows(b, g, last):
            n, _gm, par = ahead_of(b, g, 1)
            for part in range(PARTS):
                if part == 0:
                    sp.wait_ge(rows_split, n + 1)
                else:
                    wait_read(sp, *using(b, g, "rows", last))
                dst = stack[par][0][EXACT + part:EXACT + part + 1, :, :].rearrange("o h (t q) -> o (h t) q", q=P)
                sp.dma_start(dst, neg_parts[:, part, :]).then_inc(rows_stacked, 16)

        stack_parts(None, 0, False)
        stack_rows(None, 0, False)
        stack_parts(None, 1, False)

        def body(b, last):
            for g in range(GROUPS):
                if not (last and g == GROUPS - 1):
                    stack_rows(b, g, last)
                if not (last and g >= GROUPS - 2):
                    stack_parts(b, g, last)
                if g == 0:
                    if not last:
                        sp.dma_start(x_next[:], ins["xT"][bass.ds(b + 1, 1)].rearrange("o f s -> (o f) s"))\
                          .then_inc(x_next_loaded, 16)
                    sp.dma_start(x_here[:], ins["xT"][bass.ds(b, 1)].rearrange("o f s -> (o f) s"))\
                      .then_inc(x_here_loaded, 16)

        looped(sp, body)

    @block.tensor
    def _(pe):
        pe.wait_ge(weights_loaded, 16 * LOADS_W)
        for half in range(2):
            buf, _k = prologue_use(f"fold{half}")
            for hh in range(8):
                h = 8 * half + hh
                for j in range(3):
                    o = wide[buf][:, 512 * (hh // 4) + 96 * (hh % 4) + HD * j:][:, 0:HD]
                    mm = nc.tensor.matmul(o, wl[:, h, :], w3[:, j, h, :], start=True, stop=True)
            mm.then_inc(wide_full[buf], 1)
        buf, k = prologue_use("bias")
        wait_empty(pe, buf, k)
        for j in range(3):
            for h in range(HEADS):
                hh, col = h % HG, j * GROUPS + h // HG
                mm = nc.tensor.matmul(wide[buf][HD * hh:HD * hh + HD, col:col + 1], w3[:, j, h, :],
                                      blT[:, h:h + 1], start=True, stop=True)
        mm.then_inc(wide_full[buf], 1)
        buf, k = prologue_use("outbias")
        wait_empty(pe, buf, k)
        pe.wait_ge(bias_spread, GROUPS)
        for g in range(GROUPS):
            mm = nc.tensor.matmul(wide[buf][:, 0:D], bv_wide[:, g, :], woT[:, g, :],
                                  start=(g == 0), stop=(g == GROUPS - 1))
        mm.then_inc(wide_full[buf], 1)
        pe.wait_ge(setup_done, SETUP_OPS)
        for half in range(2):
            wait_read(pe, *prologue_use(f"fold{half}"))

        def embed(b, g, last):
            buf, k = using(b, g, "embed", last)
            wait_empty(pe, buf, k)
            pe.wait_ge(x_next_loaded, 16 if b is None else 16 * (b + 2))
            for c in range(2):
                mm = nc.tensor.matmul(wide[buf][:, CHUNK * c:CHUNK * (c + 1)], wtok[:],
                                      x_next[:, CHUNK * c:CHUNK * (c + 1)], start=True, stop=True)
            mm.then_inc(wide_full[buf], 1)

        def project(b, g, j, last):
            name = "v" if j == 2 else operand(b, g, j)
            buf, k = using(b, g, name, last)
            _n, gm, _par = ahead_of(b, g, 1 if j == 2 else 2)
            if j == 0 and gm == 0:
                wait_read(pe, *using(b, g, "embed", last))
            wait_empty(pe, buf, k)
            w = wqkv[:, j, P * gm:P * (gm + 1)]
            if j < 2:
                for c in range(2):
                    mm = nc.tensor.matmul(wide[buf][:, CHUNK * c:CHUNK * (c + 1)], w,
                                          h0T[:, CHUNK * c:CHUNK * (c + 1)], start=True, stop=True)
            else:
                for t in range(QT):
                    mm = nc.tensor.matmul(wide[buf][:, P * t:P * (t + 1)], h0T[:, P * t:P * (t + 1)], w,
                                          start=True, stop=True)
            mm.then_inc(wide_full[buf], 1)

        def max_scores(b, g, piece, last):
            qt, heads = piece
            buf, k = using(b, g, ("max",) + piece, last)
            _n, _gm, par = ahead_of(b, g, 1)
            if piece == PIECES[0]:
                pe.wait_ge(stacked[par], STACK_INC * (1 + same_parity_before(b, g, 1)))
            wait_empty(pe, buf, k)
            qs, ks = stack[par]
            width = P * (qt + 1)
            for x, h in enumerate(heads):
                at = piece_column(qt, x)
                lhsT = qs[0:EXACT, h, P * qt:P * (qt + 1)]
                for k0 in range(0, width, CHUNK):
                    w = min(CHUNK, width - k0)
                    diagonal = k0 + w == width
                    nc.tensor.matmul(wide[buf][:, at + k0:at + k0 + w], lhsT, ks[0:EXACT, h, k0:k0 + w],
                                     start=True, stop=not diagonal)
                mm = nc.tensor.matmul(wide[buf][:, at + width - P:at + width], ident16, above,
                                      start=False, stop=True)
            mm.then_inc(wide_full[buf], 1)

        def turn_maxima(b, g, last):
            buf, k = using(b, g, "rows", last)
            wait_empty(pe, buf, k)
            wait_read(pe, *using(b, g, ("max",) + PIECES[-2], last))
            wait_read(pe, *using(b, g, ("max",) + PIECES[-1], last))
            nc.tensor.transpose(wide[buf][0:HG * QT, 0:P], maxima[:].rearrange("p h t -> p (h t)"), ident)\
              .then_inc(wide_full[buf], 1)

        def key_scores(b, g, u, h):
            c, kt = UNITS[u]
            q0, w = unit_span(c, kt)
            par, n = g % 2, GROUPS * b + g
            qs, ks = stack[par]
            e = score[h % 2]
            if u == 0 and h == 0:
                pe.wait_ge(rows_stacked, ROWS_INC * (n + 1))
            pe.wait_ge(exponentials, 48 * n + HG * u + h + 1)
            diagonal = P * kt >= CHUNK * c
            mm = nc.tensor.matmul(e[:, 0:w], ks[0:EXACT + PARTS, h, P * kt:P * (kt + 1)],
                                  qs[0:EXACT + PARTS, h, q0:q0 + w], start=True, stop=not diagonal)
            if diagonal:
                mm = nc.tensor.matmul(e[:, 0:P], ident16, below, start=False, stop=True)
            mm.then_inc(score_full, 1)

        def mix(b, g, u):
            c, kt = UNITS[u]
            q0, w = unit_span(c, kt)
            off = q0 - CHUNK * c
            n = GROUPS * b + g
            first, final = kt == 0, P * (kt + 1) == CHUNK * (c + 1)
            if first:
                pe.wait_ge(mixed_free[c], n + 1)
            pe.wait_ge(exponentials, 2 + 48 * n + HG * (u + 1))
            for h in range(HG):
                rows = slice(HD * h, HD * h + HD)
                mm = nc.tensor.matmul(mixed[c][rows, off:off + w], values[g % 2][:, kt, rows],
                                      probs[u % RING][:, h, 0:w], start=first, stop=final)
            mm.then_inc(mixes, 1)

        def total(b, g, c, last):
            n = GROUPS * b + g
            buf, k = loop_use(b, g, f"total{c}", last)
            wait_empty(pe, buf, k)
            pe.wait_ge(pool_sums, RING + 12 * n + (4, 12)[c])
            pe.wait_ge(dve_sums, RING + 12 * n + (4, 12)[c])
            for h in range(HG):
                mm = nc.tensor.matmul(wide[buf][HD * h:HD * h + HD, 0:CHUNK], ones[:], sums[c][:, h, :],
                                      start=True, stop=True)
            mm.then_inc(wide_full[buf], 1)

        def out_map(b, last):
            buf, k = loop_use(b, GROUPS - 1, "out", last)
            wait_empty(pe, buf, k)
            pe.wait_ge(x_here_loaded, 16 * (b + 1))
            for t in range(QT):
                if P * t % CHUNK == 0:
                    pe.wait_ge(mixed_free[P * t // CHUNK], 1 + GROUPS * (b + 1))
                cols = slice(P * t, P * (t + 1))
                for g in range(GROUPS):
                    nc.tensor.matmul(wide[buf][:, cols], catT[:, g, cols], woT[:, g, :], start=(g == 0), stop=False)
                mm = nc.tensor.matmul(wide[buf][:, cols], x_here[:, cols], wtok[:], start=False, stop=True)
            mm.then_inc(wide_full[buf], 1)

        embed(None, 0, False)
        for j in range(3):
            project(None, 0, j, False)
        for piece in PIECES:
            max_scores(None, 0, piece, False)
        turn_maxima(None, 0, False)
        for j in range(2):
            project(None, 1, j, False)

        def body(b, last):
            for g in range(GROUPS):
                one, two = not (last and g >= GROUPS - 1), not (last and g >= GROUPS - 2)
                for u in range(len(UNITS)):
                    todo = list(pieces_at(u)) if one else []
                    for h in range(HG):
                        key_scores(b, g, u, h)
                        if todo:
                            max_scores(b, g, todo.pop(0), last)
                    if u >= 1:
                        mix(b, g, u - 1)
                    if u == VALUES_AT and one:
                        project(b, g, 2, last)
                    if u == TOTAL1_AT and g > 0:
                        total(b, g - 1, 1, last)
                    if u == PROJECT_AT and two:
                        if g == GROUPS - 2:
                            embed(b, g, last)
                        project(b, g, 0, last)
                        project(b, g, 1, last)
                    if u == ROWS_AT and one:
                        turn_maxima(b, g, last)
                    if u == TOTAL0_AT:
                        total(b, g, 0, last)
                mix(b, g, len(UNITS) - 1)
            total(b, GROUPS - 1, 1, last)
            out_map(b, last)

        looped(pe, body)

    @block.scalar
    def _(act):
        for half in range(2):
            buf, k = prologue_use(f"fold{half}")
            act.wait_ge(wide_full[buf], k + 1)
            src = wide[buf][:].rearrange("p (a r) -> p a r", a=2)[:, :, 0:384]\
                .rearrange("p a (h j d) -> p a h j d", h=4, j=3)
            for j in range(3):
                for a in range(2):
                    dst = wqkv[:, j, 256 * half + 128 * a:256 * half + 128 * (a + 1)]
                    final = j == 2 and a == 1
                    nc.scalar.copy(dst.rearrange("p (h d) -> p h d", h=4), src[:, a, :, j, :])\
                      .then_inc(wide_free[buf] if final else copied, 1)

        def round_operand(b, g, i, last):
            buf, k = using(b, g, operand(b, g, i), last)
            n, gm, _par = ahead_of(b, g, 2)
            if b is not None or g == 1:
                before = (g + 1) % 2
                act.wait_ge(stacked[before], STACK_INC * (1 + (0 if b is None else same_parity_before(b, g, 1))))
            act.wait_ge(wide_full[buf], k + 1)
            bcol = bias[:, i * GROUPS + gm:i * GROUPS + gm + 1]
            nc.scalar.activation(parts[i][:, 0, :], wide[buf][:], ACT.Identity, bias=bcol).then_inc(rounded, 1)

        def copy_values(b, g, last):
            buf, k = using(b, g, "v", last)
            _n, _gm, par = ahead_of(b, g, 1)
            act.wait_ge(wide_full[buf], k + 1)
            nc.scalar.copy(values[par][:].rearrange("p t c -> p (t c)"), wide[buf][:]).then_inc(wide_free[buf], 1)

        wait_read(act, *prologue_use("bias"))
        for i in range(2):
            round_operand(None, 0, i, False)
        copy_values(None, 0, False)
        for i in range(2):
            round_operand(None, 1, i, False)

        def body(b, last):
            for g in range(GROUPS):
                n = GROUPS * b + g
                one, two = not (last and g >= GROUPS - 1), not (last and g >= GROUPS - 2)
                for u in range(len(UNITS)):
                    _q0, w = unit_span(*UNITS[u])
                    act.wait_ge(mixes, 12 * n + u + 1)
                    act.wait_ge(pool_sums, 12 * n + u + 1)
                    act.wait_ge(dve_sums, 12 * n + u + 1)
                    for h in range(HG):
                        act.wait_ge(score_full, 48 * n + HG * u + h + 1)
                        nc.scalar.activation(probs[u % RING][:, h, 0:w], score[h % 2][:, 0:w], ACT.Exp)\
                          .then_inc(exponentials, 1)
                    if u == VALUES_AT and one:
                        copy_values(b, g, last)
                    if u == PROJECT_AT and two:
                        round_operand(b, g, 0, last)
                        round_operand(b, g, 1, last)
            act.wait_ge(moments_ready, 2 * QT * (b + 1))
            nc.scalar.activation(rstd[:], moments[:, :, 1], ACT.Sqrt, bias=eps[:, 0:1]).then_inc(deviation, 1)

        looped(act, body)

    @block.gpsimd
    def _(pool):
        def body(b, last):
            for g in range(GROUPS):
                for u in range(len(UNITS)):
                    add_up(pool, nc.gpsimd, pool_sums, b, g, u, 0, POOL_HEADS)

        looped(pool, body)

    @block.vector
    def _(dve):
        nc.vector.memset(ones[:], 1.0).then_inc(setup_done, 1)
        nc.vector.memset(eps[:], EPS).then_inc(setup_done, 1)
        nc.vector.memset(bv_wide, 0.0).then_inc(setup_done, 1)
        dve.sem_inc(exponentials, 2)
        for start_free in (mixes, pool_sums, dve_sums):
            dve.sem_inc(start_free, RING)
        for c in range(2):
            dve.sem_inc(mixed_free[c], 1)
        for par in range(2):
            nc.vector.memset(stack[par][1][EXACT:EXACT + PARTS, :, :], MAX_UNIT).then_inc(setup_done, 1)
        dve.wait_ge(consts_loaded, 16 * LOADS_C)
        nc.vector.tensor_copy(cst16[:], cst[:]).then_inc(setup_done, 1)
        buf, k = prologue_use("bias")
        dve.wait_ge(wide_full[buf], k + 1)
        nc.vector.tensor_copy(bias[:], wide[buf][:, 0:3 * GROUPS]).then_inc(wide_free[buf], 1)
        wait_read(dve, buf, k)
        dve.wait_ge(setup_done, 6)
        for g in range(GROUPS):
            nc.vector.tensor_scalar(bv_wide[:, g, :], bv_wide[:, g, :], bias[:, 2 * GROUPS + g:2 * GROUPS + g + 1],
                                    None, ALU.add).then_inc(bias_spread, 1)
        buf, k = prologue_use("outbias")
        dve.wait_ge(wide_full[buf], k + 1)
        dve.wait_ge(weights_loaded, 16 * LOADS_W)
        nc.vector.tensor_tensor(bo[:], bo[:], wide[buf][:, 0:D], ALU.add).then_inc(wide_free[buf], 1)
        wait_read(dve, buf, k)
        nc.vector.tensor_tensor(peb[:], peb[:], bo[:, None, :].broadcast_to([P, QT, D]), ALU.add)\
          .then_inc(setup_done, 1)
        dve.wait_ge(setup_done, SETUP_OPS)

        def add_positions(b, g, last):
            buf, k = using(b, g, "embed", last)
            dve.wait_ge(wide_full[buf], k + 1)
            nc.vector.tensor_tensor(h0T[:], wide[buf][:], peT[:], ALU.add).then_inc(wide_free[buf], 1)

        def low_part(b, g, i, last):
            buf, k = using(b, g, operand(b, g, i), last)
            n, gm, _par = ahead_of(b, g, 2)
            dve.wait_ge(rounded, 2 * n + i + 1)
            bcol = bias[:, i * GROUPS + gm:i * GROUPS + gm + 1]
            nc.vector.scalar_tensor_tensor(parts[i][:, 1, :], wide[buf][:], bcol, parts[i][:, 0, :], ALU.add,
                                           ALU.subtract).then_inc(wide_free[buf], 1)

        def piece_max(b, g, piece, last):
            qt, heads = piece
            buf, k = using(b, g, ("max",) + piece, last)
            width, n = P * (qt + 1), len(heads)
            dve.wait_ge(wide_full[buf], k + 1)
            if n == 4 and qt == 1:
                src = wide[buf][:].rearrange("p (h w) -> p h w", h=4)
            elif n == 4:
                src = wide[buf][:, 0:CHUNK].rearrange("p (h w) -> p h w", h=4)
            elif n == 2:
                src = wide[buf][:].rearrange("p (h w) -> p h w", h=2)[:, :, 0:width]
            else:
                src = wide[buf][:, None, 0:width]
            nc.vector.tensor_reduce(maxima[:, heads[0]:heads[0] + n, qt], src, AX_X, ALU.max)\
              .then_inc(wide_free[buf], 1)

        def split_maxima(b, g, last):
            buf, k = using(b, g, "rows", last)
            n = ahead_of(b, g, 1)[0]
            src = wide[buf][0:HG * QT, 0:P]
            dve.wait_ge(wide_full[buf], k + 1)
            if b is not None:
                dve.wait_ge(rows_stacked, ROWS_INC * n)
            nc.vector.tensor_scalar(neg_parts[:, 0, :], src, -1.0 / MAX_UNIT, None, ALU.mult).then_inc(rows_split, 1)
            dve.wait_ge(rows_split, n + 1)
            nc.vector.scalar_tensor_tensor(neg_parts[:, 1, :], src, -1.0 / MAX_UNIT, neg_parts[:, 0, :],
                                           ALU.mult, ALU.subtract).then_inc(wide_free[buf], 1)

        def normalise(b, g, c, last):
            n = GROUPS * b + g
            buf, k = loop_use(b, g, f"total{c}", last)
            dve.wait_ge(wide_full[buf], k + 1)
            nc.vector.reciprocal(recip[:], wide[buf][:, 0:CHUNK]).then_inc(wide_free[buf], 1)
            wait_read(dve, buf, k)
            nc.vector.tensor_tensor(catT[:, g, CHUNK * c:CHUNK * (c + 1)], mixed[c][:], recip[:], ALU.mult)\
              .then_inc(mixed_free[c], 1)

        def layernorm(b, last):
            buf, k = loop_use(b, GROUPS - 1, "out", last)
            dve.wait_ge(wide_full[buf], k + 1)
            nc.vector.tensor_tensor(y[:].rearrange("p t d -> p (t d)"), wide[buf][:],
                                    peb[:].rearrange("p t d -> p (t d)"), ALU.add).then_inc(wide_free[buf], 1)
            wait_read(dve, buf, k)
            for t in range(QT):
                nc.vector.bn_stats(stats[:, t, :], y[:, t, :]).then_inc(moments_ready, 1)
            dve.wait_ge(moments_ready, 2 * QT * b + QT)
            dve.sem_inc(passed, 1)
            for t in range(QT):
                nc.vector.bn_aggr(moments[:, t, :], stats[:, t, :]).then_inc(moments_ready, 1)
            dve.wait_ge(moments_ready, 2 * QT * (b + 1))
            nc.vector.tensor_tensor(y[:], y[:], moments[:, :, 0:1].broadcast_to([P, QT, D]), ALU.subtract)\
              .then_inc(centred, 1)
            dve.wait_ge(deviation, b + 1)
            nc.vector.reciprocal(rstd[:], rstd[:]).then_inc(rstd_ready, 1)
            dve.wait_ge(centred, b + 1)
            dve.wait_ge(rstd_ready, b + 1)
            nc.vector.tensor_tensor(h1[:, bass.ds(b * QT, QT), :], y[:],
                                    rstd[:, :, None].broadcast_to([P, QT, D]), ALU.mult).then_inc(normed, 1)

        add_positions(None, 0, False)
        for i in range(2):
            low_part(None, 0, i, False)
        for piece in PIECES:
            piece_max(None, 0, piece, False)
        split_maxima(None, 0, False)
        for i in range(2):
            low_part(None, 1, i, False)

        def body(b, last):
            for g in range(GROUPS):
                one, two = not (last and g >= GROUPS - 1), not (last and g >= GROUPS - 2)
                for u in range(len(UNITS)):
                    for piece in (pieces_at(u) if one else ()):
                        piece_max(b, g, piece, last)
                    if u >= 1:
                        add_up(dve, nc.vector, dve_sums, b, g, u - 1, POOL_HEADS, HG)
                    if u == TOTAL1_AT and g > 0:
                        normalise(b, g - 1, 1, last)
                    if u == PROJECT_AT and two:
                        if g == GROUPS - 2:
                            add_positions(b, g, last)
                        low_part(b, g, 0, last)
                        low_part(b, g, 1, last)
                    if u == ROWS_AT and one:
                        split_maxima(b, g, last)
                    if u == TOTAL0_AT:
                        normalise(b, g, 0, last)
                add_up(dve, nc.vector, dve_sums, b, g, len(UNITS) - 1, POOL_HEADS, HG)
            normalise(b, GROUPS - 1, 1, last)
            layernorm(b, last)
            dve.wait_ge(normed, b + 1)

        looped(dve, body)

    return ctx


def piece_column(qt, x):
    return (P, 2 * P, CHUNK, CHUNK, 0, 0, 0, 0)[qt] * x


TILES = B * SEQ // P
KEYS, TOPK, FH = 64, 8, 8
EXPERTS = KEYS * KEYS
BLOCKS = EXPERTS // P
SLOTS = 2 * FH
CHOSEN = FH * TOPK
CANDS = 20
HALF = P // 2
BANK_TOKENS = CHUNK // BLOCKS
BANKS = P // BANK_TOKENS
BIAS_PARTS = 3
SCALE = float(2 ** 14)
FLOOR = 12582912.0


def candidates(a, b, out):
    rows = lambda lo, hi, n: a[:, :, lo:hi, None].broadcast_to([P, FH, hi - lo, n])
    cols = lambda n, m: b[:, :, None, 0:n].broadcast_to([P, FH, m, n])
    at = lambda lo, m, n: out[:, :, lo:lo + m * n].rearrange("p h (m n) -> p h m n", m=m)
    return [(rows(0, 1, 8), cols(8, 1), at(0, 1, 8)), (rows(1, 2, 4), cols(4, 1), at(8, 1, 4)),
            (rows(2, 4, 2), cols(2, 2), at(12, 2, 2)), (rows(4, 8, 1), cols(1, 4), at(16, 4, 1))]


def feed_forward(nc, ins, h1, out, outer):
    ctx = outer.enter_context(ExitStack())

    def sb(name, shape, dt):
        return ctx.enter_context(nc.sbuf_tensor(name, shape, dt))

    def sem(name):
        return ctx.enter_context(nc.semaphore(name))

    def psum(name, shape):
        return ctx.enter_context(nc.psum_tensor(name, shape, F32))

    key_ps = psum("key_ps", [P, SLOTS * KEYS])
    turn_ps = psum("turn_ps", [P, CHUNK])
    inner_ps = psum("inner_ps", [P, 2, CHUNK])
    weight_ps = psum("weight_ps", [P, 2, CHUNK])
    up_ps = psum("up_ps", [P, CHUNK])

    down = sb("down", [P, BLOCKS, P], F32)
    up = sb("up", [P, BLOCKS, D], F32)
    wqT = up[0:KEYS, 0:SLOTS, :]
    keysT = up[0:KEYS, SLOTS:SLOTS + SLOTS // 2, :].rearrange("c a b -> c (a b)")\
        .rearrange("c (s n) -> c s n", s=SLOTS)
    bqT = up[0:KEYS, BLOCKS - 1, 0:SLOTS]
    wkey = sb("wkey", [P, SLOTS * KEYS], F32)
    bkey_row = sb("bkey_row", [1, BIAS_PARTS, SLOTS * KEYS], BF16)
    bkey_rest = sb("bkey_rest", [1, SLOTS * KEYS], F32)
    bkey = sb("bkey", [P, SLOTS * KEYS], BF16)
    ones16 = sb("ones16", [P, P], BF16)
    cst = sb("cst_ffn", [P, 2, P], F32)
    ident, iota = cst[:, 0, :], cst[:, 1, :]
    numbers = sb("numbers", [P, P, HALF], F16)
    eps = sb("eps_ffn", [P, 1], F32)

    xs = [sb(f"xs{i}", [P, D], F32) for i in range(2)]
    xT = [sb(f"xT{i}", [P, P], F32) for i in range(2)]
    keyscore = sb("keyscore", [P, SLOTS, KEYS], F32)
    tops = sb("tops", [P, FH, 2, TOPK], F32)
    ranks = sb("ranks", [P, FH, 2, TOPK], U32)
    ranksf = sb("ranksf", [P, FH, 2, TOPK], F32)
    cand = sb("cand", [P, FH, CANDS], F32)
    codes = sb("codes", [P, FH, CANDS], F32)
    best = sb("best", [P, FH, TOPK], F32)
    place = sb("place", [P, FH, TOPK], U32)
    placef = sb("placef", [P, FH, TOPK], F32)
    below_max = sb("below_max", [P, FH, TOPK], F32)
    expo = sb("expo", [P, FH, TOPK], F32)
    denom = sb("denom", [P, FH], F32)
    match = sb("match", [P, CANDS, CHOSEN], F32)
    expert = sb("expert", [P, CHOSEN], F32)
    choice = sb("choice", [P, 3, CHOSEN], F32)
    turned16 = sb("turned16", [P, 2, P], F16)
    weight16 = sb("weight16", [P, P], F16)
    row_hot = [sb(f"row_hot{i}", [P, P, HALF], F16) for i in range(2)]
    block_hot = [sb(f"block_hot{i}", [P, BLOCKS, HALF], F16) for i in range(2)]
    vals = sb("vals", [P, BLOCKS, P], F32)
    y = sb("y_ffn", [P, D], F32)
    stats = sb("stats_ffn", [P, 6], F32)
    moments = sb("moments_ffn", [P, 2], F32)
    rstd = sb("rstd_ffn", [P, 1], F32)
    result = [sb(f"result{i}", [P, D], F32) for i in range(2)]

    passed = sem("passed_ffn")
    small_loaded = sem("small_loaded")
    down_loaded = sem("down_loaded")
    up_loaded = sem("up_loaded")
    bias_loaded = sem("bias_loaded")
    ffn_setup = sem("ffn_setup")
    key_folded = sem("key_folded")
    key_copied = sem("key_copied")
    bias_parts = sem("bias_parts")
    x_copied = sem("x_copied")
    x_turned = sem("x_turned")
    xT_ready = sem("xT_ready")
    keys_scored = sem("keys_scored")
    keys_ready = sem("keys_ready")
    topped = sem("topped")
    summed = sem("summed")
    picked = sem("picked")
    coding = sem("coding")
    lowered = sem("lowered")
    matching = sem("matching")
    exponed = sem("exponed")
    deciding = sem("deciding")
    choices_turned = sem("choices_turned")
    turned_ready = sem("turned_ready")
    low_ready = sem("low_ready")
    built = sem("built")
    inner_full = sem("inner_full")
    rectified = sem("rectified")
    weight_full = sem("weight_full")
    weighted = sem("weighted")
    up_full = sem("up_full")
    added = sem("added")
    moments_done = sem("moments_done")
    deviated = sem("deviated")
    inverted = sem("inverted")
    finished = sem("finished")
    stored = [sem(f"stored{i}") for i in range(2)]
    DECIDE = 7

    def looped(eng, body):
        with eng.Fori(0, TILES // 2 - 1) as pair:
            for par in range(2):
                body(2 * pair + par, pair, par, 2)
        body(TILES - 2, TILES // 2 - 1, 0, 1)
        body(TILES - 1, TILES // 2 - 1, 1, 0)

    block = ctx.enter_context(nc.Block())

    @block.sync
    def _(sp):
        sp.dma_start(wqT, ins["WqT_ffn"]).then_inc(small_loaded, 16)
        sp.dma_start(keysT, ins["keysT"]).then_inc(small_loaded, 16)
        sp.dma_start(bqT, ins["bqT"]).then_inc(small_loaded, 16)
        sp.dma_start(cst[:], ins["cst_ffn"]).then_inc(small_loaded, 16)
        sp.dma_start(down[:], ins["downT"].rearrange("d (n e) -> d n e", e=P)).then_inc(down_loaded, 16)
        sp.wait_ge(bias_parts, 4)
        for part in range(BIAS_PARTS):
            sp.dma_start(bkey[part:part + 1, :], bkey_row[:, part, :]).then_inc(bias_loaded, 16)
        sp.wait_ge(key_folded, 2)
        sp.dma_start(up[:], ins["up"].rearrange("(n e) d -> e n d", e=P)).then_inc(up_loaded, 16)

        def body(i, pair, par, ahead):
            sp.wait_ge(finished, i + 1)
            dst = out[bass.ds(i, 1)] if not isinstance(i, int) else out[i:i + 1]
            sp.dma_start(dst.rearrange("o p d -> (o p) d"), result[par][:]).then_inc(stored[par], 16)

        looped(sp, body)
        for par in range(2):
            sp.wait_ge(stored[par], 16 * (TILES // 2 + 1))

    @block.tensor
    def _(pe):
        pe.wait_ge(small_loaded, 16 * 4)
        for s in range(SLOTS):
            mm = nc.tensor.matmul(key_ps[:, KEYS * s:KEYS * (s + 1)], wqT[:, s, :], keysT[:, s, :],
                                  start=True, stop=True)
        mm.then_inc(key_folded, 1)
        flat = weight_ps[:].rearrange("p a b -> p (a b)")
        for s in range(SLOTS):
            mm = nc.tensor.matmul(flat[0:1, KEYS * s:KEYS * (s + 1)], bqT[:, s:s + 1], keysT[:, s, :],
                                  start=True, stop=True)
        mm.then_inc(key_folded, 1)
        pe.wait_ge(key_copied, 1)
        pe.wait_ge(ffn_setup, 5)
        pe.wait_ge(bias_loaded, 16 * BIAS_PARTS)

        def turn_tokens(j, par):
            pe.wait_ge(x_copied, j + 1)
            pe.wait_ge(keys_ready, j)
            nc.tensor.transpose(key_ps[:, 0:P], xs[par][:], ident).then_inc(x_turned, 1)

        def score_keys(j, par):
            pe.wait_ge(xT_ready, j + 1)
            for c in range(2):
                cols = slice(CHUNK * c, CHUNK * (c + 1))
                nc.tensor.matmul(key_ps[:, cols], xT[par][:], wkey[:, cols], start=True, stop=False)
                mm = nc.tensor.matmul(key_ps[:, cols], ones16[:], bkey[:, cols], start=False, stop=True)
            mm.then_inc(keys_scored, 1)

        def turn_choices(j):
            pe.wait_ge(deciding, DECIDE * (j + 1))
            pe.wait_ge(low_ready, j)
            for k in range(3):
                for twice in range(2):
                    mm = nc.tensor.matmul(turn_ps[CHOSEN * twice:CHOSEN * (twice + 1), P * k:P * (k + 1)],
                                          choice[:, k, :], ident, start=True, stop=True)
            mm.then_inc(choices_turned, 1)

        def inner(i, par):
            for k in range(BANKS):
                pe.wait_ge(rectified, BANKS * i + k + 1)
                for n in range(4 * k, 4 * k + 4):
                    mm = nc.tensor.matmul(inner_ps[:, k % 2, P * (n % 4):P * (n % 4 + 1)], down[:, n, :], xT[par][:],
                                          start=True, stop=True)
                mm.then_inc(inner_full, 1)

        def expert_weights(i):
            for k in range(BANKS):
                half = k // (BANKS // 2)
                if k % (BANKS // 2) == 0:
                    pe.wait_ge(built, 6 * i + 3 * (half + 1))
                pe.wait_ge(weighted, BANKS * i + k + 1)
                for s in range(BANK_TOKENS):
                    t = BANK_TOKENS * k + s - HALF * half
                    mm = nc.tensor.matmul(weight_ps[:, k % 2, BLOCKS * s:BLOCKS * (s + 1)],
                                          row_hot[half][:, :, t], block_hot[half][:, :, t], start=True, stop=True)
                mm.then_inc(weight_full, 1)

        def up_product(i):
            pe.wait_ge(weighted, 2 + BANKS * (i + 1))
            pe.wait_ge(added, i + 1)
            for n in range(BLOCKS):
                mm = nc.tensor.matmul(up_ps[:, 0:D], vals[:, n, :], up[:, n, :],
                                      start=(n == 0), stop=(n == BLOCKS - 1))
            mm.then_inc(up_full, 1)

        turn_tokens(0, 0)
        score_keys(0, 0)
        turn_choices(0)
        turn_tokens(1, 1)
        score_keys(1, 1)
        pe.wait_ge(down_loaded, 16)
        pe.wait_ge(up_loaded, 16)

        def body(i, pair, par, ahead):
            inner(i, par)
            if ahead == 2:
                turn_tokens(i + 2, par)
                score_keys(i + 2, par)
            if ahead:
                turn_choices(i + 1)
            expert_weights(i)
            up_product(i)

        looped(pe, body)

    @block.scalar
    def _(act):
        act.wait_ge(key_folded, 1)
        nc.scalar.copy(wkey[:], key_ps[:]).then_inc(key_copied, 1)

        def copy_tokens(j, par):
            act.wait_ge(x_turned, j + 1)
            nc.scalar.copy(xT[par][:], key_ps[:, 0:P]).then_inc(xT_ready, 1)

        def copy_keys(j):
            act.wait_ge(topped, 2 * j)
            act.wait_ge(keys_scored, j + 1)
            nc.scalar.copy(keyscore[:].rearrange("p s n -> p (s n)"), key_ps[:]).then_inc(keys_ready, 1)

        def exponentiate(j):
            act.wait_ge(lowered, j + 1)
            act.wait_ge(deciding, DECIDE * j)
            nc.scalar.activation(expo[:], below_max[:], ACT.Exp).then_inc(exponed, 1)

        def copy_choices(j):
            act.wait_ge(built, 6 * j)
            act.wait_ge(choices_turned, j + 1)
            nc.scalar.copy(turned16[:].rearrange("p a t -> p (a t)"), turn_ps[:, 0:2 * P]).then_inc(turned_ready, 1)
            nc.scalar.copy(weight16[:], turn_ps[:, 2 * P:3 * P]).then_inc(turned_ready, 1)

        def rectify(i):
            for k in range(BANKS):
                act.wait_ge(inner_full, BANKS * i + k + 1)
                nc.scalar.activation(vals[:, 4 * k:4 * k + 4, :].rearrange("p n t -> p (n t)"), inner_ps[:, k % 2, :],
                                     ACT.Relu, scale=1.0 / SCALE).then_inc(rectified, 1)

        def deviate(i):
            act.wait_ge(moments_done, 2 * (i + 1))
            nc.scalar.activation(rstd[:], moments[:, 1:2], ACT.Sqrt, bias=eps[:, 0:1]).then_inc(deviated, 1)

        copy_tokens(0, 0)
        copy_keys(0)
        exponentiate(0)
        copy_choices(0)
        copy_tokens(1, 1)
        copy_keys(1)
        exponentiate(1)

        def body(i, pair, par, ahead):
            rectify(i)
            if ahead == 2:
                copy_tokens(i + 2, par)
                copy_keys(i + 2)
            if ahead:
                copy_choices(i + 1)
            if ahead == 2:
                exponentiate(i + 2)
            deviate(i)

        looped(act, body)

    @block.gpsimd
    def _(pool):
        def copy_x(j, par, late):
            if late:
                pool.wait_ge(x_turned, j - 1)
                pool.sem_inc(passed, 1)
            src = h1[:, bass.ds(j, 1), :] if not isinstance(j, int) else h1[:, j:j + 1, :]
            nc.gpsimd.tensor_copy(xs[par][:, None, :], src).then_inc(x_copied, 1)

        def decode(j):
            pool.wait_ge(topped, 2 * (j + 1))
            pool.sem_inc(passed, 1)
            nc.gpsimd.tensor_copy(ranksf[:], ranks[:]).then_inc(coding, 1)
            pool.wait_ge(coding, 3 * j + 1)
            pool.sem_inc(passed, 1)
            nc.gpsimd.tensor_scalar(ranksf[:, :, 0, :], ranksf[:, :, 0, :], float(KEYS), None, ALU.mult)\
              .then_inc(coding, 1)
            pool.wait_ge(coding, 3 * j + 2)
            ops = candidates(ranksf[:, :, 0, :], ranksf[:, :, 1, :], codes)
            for a, b, o in ops:
                last = nc.gpsimd.tensor_tensor(o, a, b, ALU.add)
            last.then_inc(coding, 1)
            pool.wait_ge(picked, 2 * (j + 1))
            pool.wait_ge(exponed, j)
            nc.gpsimd.tensor_tensor(below_max[:], best[:], best[:, :, 0:1].broadcast_to([P, FH, TOPK]),
                                    ALU.subtract).then_inc(lowered, 1)
            nc.gpsimd.tensor_copy(placef[:], place[:]).then_inc(matching, 1)
            pool.wait_ge(matching, 3 * j + 1)
            pool.wait_ge(deciding, DECIDE * j)
            pool.sem_inc(passed, 1)
            flat = placef[:].rearrange("p h k -> p (h k)")
            for c in range(CANDS):
                last = nc.gpsimd.tensor_scalar(match[:, c, :], flat, float(c), None, ALU.is_equal)
            last.then_inc(matching, 1)
            pool.wait_ge(matching, 3 * j + 2)
            pool.wait_ge(coding, 3 * j + 3)
            view = match[:].rearrange("p c (h k) -> p c h k", h=FH)
            per_cand = codes[:].rearrange("p h c -> p c h")[:, :, :, None].broadcast_to([P, CANDS, FH, TOPK])
            nc.gpsimd.tensor_tensor(view, view, per_cand, ALU.mult).then_inc(matching, 1)

        copy_x(0, 0, False)
        copy_x(1, 1, False)
        pool.wait_ge(ffn_setup, 5)
        decode(0)
        decode(1)

        def body(i, pair, par, ahead):
            if ahead == 2:
                copy_x(i + 2, par, True)
                decode(i + 2)

        looped(pool, body)

    @block.vector
    def _(dve):
        dve.sem_inc(rectified, 2)
        dve.sem_inc(weighted, 2)
        dve.sem_inc(added, 1)
        for par in range(2):
            dve.sem_inc(stored[par], 16)
        nc.vector.memset(ones16[:], 1.0).then_inc(ffn_setup, 1)
        nc.vector.memset(eps[:], EPS).then_inc(ffn_setup, 1)
        nc.vector.memset(bkey[:], 0.0).then_inc(ffn_setup, 1)
        dve.wait_ge(ffn_setup, 3)
        dve.wait_ge(small_loaded, 16 * 4)
        nc.vector.tensor_copy(numbers[:], iota[:, :, None].broadcast_to([P, P, HALF])).then_inc(ffn_setup, 1)
        dve.wait_ge(key_folded, 2)
        src = weight_ps[0:1, :, :].rearrange("p a b -> p (a b)")
        nc.vector.tensor_copy(bkey_row[:, 0, :], src).then_inc(bias_parts, 1)
        dve.wait_ge(bias_parts, 1)
        nc.vector.tensor_tensor(bkey_rest[:], src, bkey_row[:, 0, :], ALU.subtract).then_inc(bias_parts, 1)
        dve.wait_ge(bias_parts, 2)
        nc.vector.tensor_copy(bkey_row[:, 1, :], bkey_rest[:]).then_inc(bias_parts, 1)
        dve.wait_ge(bias_parts, 3)
        nc.vector.tensor_tensor(bkey_row[:, 2, :], bkey_rest[:], bkey_row[:, 1, :], ALU.subtract)\
          .then_inc(bias_parts, 1)
        dve.wait_ge(bias_parts, 4)
        nc.vector.memset(denom[:], 0.0).then_inc(ffn_setup, 1)
        dve.wait_ge(ffn_setup, 5)

        def search(j):
            dve.wait_ge(keys_ready, j + 1)
            dve.wait_ge(matching, 3 * j)
            dve.sem_inc(passed, 1)
            for s in range(SLOTS):
                last = nc.vector.max(tops[:, s // 2, s % 2, :], keyscore[:, s, :])
            last.then_inc(topped, 1)
            dve.wait_ge(topped, 2 * j + 1)
            dve.sem_inc(passed, 1)
            for s in range(SLOTS):
                last = nc.vector.max_index(ranks[:, s // 2, s % 2, :], tops[:, s // 2, s % 2, :], keyscore[:, s, :])
            last.then_inc(topped, 1)
            for a, b, o in candidates(tops[:, :, 0, :], tops[:, :, 1, :], cand):
                last = nc.vector.tensor_tensor(o, a, b, ALU.add)
            last.then_inc(summed, 1)
            dve.wait_ge(summed, j + 1)
            dve.sem_inc(passed, 1)
            for h in range(FH):
                last = nc.vector.max(best[:, h, :], cand[:, h, :])
            last.then_inc(picked, 1)
            dve.wait_ge(picked, 2 * j + 1)
            dve.sem_inc(passed, 1)
            for h in range(FH):
                last = nc.vector.max_index(place[:, h, :], best[:, h, :], cand[:, h, :])
            last.then_inc(picked, 1)

        def decide(j):
            n = DECIDE * j
            dve.wait_ge(matching, 3 * (j + 1))
            dve.wait_ge(choices_turned, j)
            nc.vector.tensor_reduce(expert[:], match[:].rearrange("p c x -> p x c"), AX_X, ALU.add)\
              .then_inc(deciding, 1)
            dve.wait_ge(exponed, j + 1)
            nc.vector.tensor_reduce(denom[:], expo[:], AX_X, ALU.add).then_inc(deciding, 1)
            dve.wait_ge(deciding, n + 1)
            nc.vector.tensor_scalar(choice[:, 1, :], expert[:], 1.0 / P, 0.5 - 0.5 / P, ALU.mult, ALU.subtract)\
              .then_inc(deciding, 1)
            dve.wait_ge(deciding, n + 2)
            nc.vector.reciprocal(denom[:], denom[:]).then_inc(deciding, 1)
            dve.wait_ge(deciding, n + 3)
            nc.vector.tensor_scalar(choice[:, 1, :], choice[:, 1, :], FLOOR, FLOOR, ALU.add, ALU.subtract)\
              .then_inc(deciding, 1)
            dve.wait_ge(deciding, n + 4)
            nc.vector.scalar_tensor_tensor(choice[:, 2, :].rearrange("p (h k) -> p h k", h=FH), expo[:], SCALE,
                                           denom[:, :, None].broadcast_to([P, FH, TOPK]), ALU.mult, ALU.mult)\
              .then_inc(deciding, 1)
            dve.wait_ge(deciding, n + 5)
            nc.vector.scalar_tensor_tensor(choice[:, 0, :], choice[:, 1, :], -float(P), expert[:], ALU.mult, ALU.add)\
              .then_inc(deciding, 1)

        def low_parts(j):
            dve.wait_ge(turned_ready, 2 * (j + 1))
            low = weight16[CHOSEN:P, :]
            nc.vector.tensor_tensor(low, turn_ps[CHOSEN:P, 2 * P:3 * P], low, ALU.subtract).then_inc(low_ready, 1)
            dve.wait_ge(low_ready, j + 1)

        def build(j, late):
            for half in range(2):
                cols = slice(HALF * half, HALF * (half + 1))
                if late:
                    dve.wait_ge(weight_full, BANKS * (j - 1) + (BANKS // 2) * (half + 1))

                def over(n, src):
                    return src[:, None, cols].broadcast_to([P, n, HALF])

                nc.vector.tensor_tensor(block_hot[half][:], numbers[:, 0:BLOCKS, :], over(BLOCKS, turned16[:, 1, :]),
                                        ALU.is_equal).then_inc(built, 1)
                nc.vector.tensor_tensor(row_hot[half][:], numbers[:], over(P, turned16[:, 0, :]),
                                        ALU.is_equal).then_inc(built, 1)
                dve.wait_ge(built, 6 * j + 3 * half + 1)
                nc.vector.tensor_tensor(block_hot[half][:], block_hot[half][:], over(BLOCKS, weight16),
                                        ALU.mult).then_inc(built, 1)

        def weigh(i):
            dve.wait_ge(rectified, 2 + BANKS * (i + 1))
            for k in range(BANKS):
                v = vals[:, :, BANK_TOKENS * k:BANK_TOKENS * (k + 1)]
                dve.wait_ge(weight_full, BANKS * i + k + 1)
                nc.vector.tensor_tensor(v, weight_ps[:, k % 2, :].rearrange("p (t n) -> p n t", n=BLOCKS), v,
                                        ALU.mult).then_inc(weighted, 1)

        def moments_of(i):
            dve.wait_ge(up_full, i + 1)
            here = h1[:, bass.ds(i, 1), :] if not isinstance(i, int) else h1[:, i:i + 1, :]
            nc.vector.tensor_tensor(y[:, None, :], up_ps[:, None, 0:D], here, ALU.add).then_inc(added, 1)
            dve.wait_ge(added, i + 2)
            nc.vector.bn_stats(stats[:], y[:]).then_inc(moments_done, 1)
            dve.wait_ge(moments_done, 2 * i + 1)
            dve.sem_inc(passed, 1)
            nc.vector.bn_aggr(moments[:], stats[:]).then_inc(moments_done, 1)

        def finish(i, pair, par):
            dve.wait_ge(deviated, i + 1)
            nc.vector.reciprocal(rstd[:], rstd[:]).then_inc(inverted, 1)
            dve.wait_ge(inverted, i + 1)
            dve.wait_ge(stored[par], 16 * (pair + 1))
            nc.vector.tensor_scalar(result[par][:], y[:], moments[:, 0:1], rstd[:, 0:1], ALU.subtract, ALU.mult)\
              .then_inc(finished, 1)
            dve.wait_ge(finished, i + 1)

        search(0)
        decide(0)
        search(1)
        low_parts(0)
        build(0, False)

        def body(i, pair, par, ahead):
            if ahead:
                decide(i + 1)
            weigh(i)
            if ahead == 2:
                search(i + 2)
            moments_of(i)
            if ahead:
                low_parts(i + 1)
                build(i + 1, True)
            finish(i, pair, par)

        looped(dve, body)

    return ctx


def positions():
    position = np.arange(SEQ * 2, dtype=np.float32)[:, None]
    div_term = np.exp(np.arange(0, D, 2, dtype=np.float32) * (-np.log(10000.0) / D)).astype(np.float32)
    pe = np.zeros((SEQ * 2, D), dtype=np.float32)
    pe[:, 0::2] = np.sin(position * div_term)
    pe[:, 1::2] = np.cos(position * div_term)
    return pe[:SEQ]


FFN_INS = ["WqT_ffn", "keysT", "bqT", "cst_ffn", "downT", "up"]
ATT_INS = ["xT", "Wtok", "Wl", "blT", "Wq", "Wk", "Wv", "WoT", "bo", "pe", "peT", "cst"]


def host_arrays(**a):
    def lay(x):
        return np.ascontiguousarray(x)
    above = np.triu(np.full((P, P), -1e30, np.float32), 1)
    pe = positions()
    return {
        "xT": lay(np.asarray(a["x"]).reshape(B, SEQ, FEAT).transpose(0, 2, 1)),
        "Wtok": lay(a["L0_tok_W"]),
        "Wl": lay(a["L0_attn_Wl"]),
        "blT": lay(np.asarray(a["L0_attn_bl"]).T),
        "Wq": lay(a["L0_attn_Wq"]), "Wk": lay(a["L0_attn_Wk"]), "Wv": lay(a["L0_attn_Wv"]),
        "WoT": lay(np.asarray(a["L0_attn_Wo"]).T),
        "bo": lay(a["L0_attn_bo"]),
        "pe": pe, "peT": lay(pe.T),
        "WqT_ffn": lay(np.asarray(a["L0_ffn_Wq"]).reshape(D, SLOTS, KEYS).transpose(2, 1, 0)),
        "keysT": lay(np.asarray(a["L0_ffn_keys"]).reshape(SLOTS, KEYS, KEYS).transpose(2, 0, 1)),
        "bqT": lay(np.asarray(a["L0_ffn_bq"]).reshape(SLOTS, KEYS).T),
        "cst_ffn": lay(np.stack([np.eye(P, dtype=np.float32), np.tile(np.arange(P, dtype=np.float32), (P, 1))], 1)),
        "downT": lay(np.asarray(a["L0_ffn_w_down"]).T),
        "up": lay(a["L0_ffn_w_up"]),
        "cst": lay(np.stack([np.eye(P, dtype=np.float32), above, above.T], 1)),
    }


def vit_layer(nc, ins, out):
    with ExitStack() as ctx:
        h1 = ctx.enter_context(nc.sbuf_tensor("h1", [P, TILES, D], F32))
        with ExitStack() as first:
            attention(nc, ins, h1, first)
        with ExitStack() as second:
            feed_forward(nc, ins, h1, out, second)


def kernel(**inputs):
    import numpy as _np
    import concourse.bacc as _bacc
    from concourse import mybir as _mybir
    from concourse.bass_utils import run_bass_kernel_spmd as _run

    nc = _bacc.Bacc("TRN2", target_bir_lowering=False, num_devices=1)
    arrays, ins = {}, {}
    for name, a in host_arrays(**inputs).items():
        arrays[f"in_{name}_dram"] = a
        ins[name] = nc.dram_tensor(f"in_{name}_dram", a.shape, _mybir.dt.from_np(a.dtype), kind="ExternalInput").ap()
    out = nc.dram_tensor("out_dram", (TILES, P, D), _mybir.dt.float32, kind="ExternalOutput").ap()
    vit_layer(nc, ins, out)
    r = _run(nc, [arrays], core_ids=[0])
    return _np.asarray(r.results[0]["out_dram"]).reshape(B, SEQ, D)
```

```python
from contextlib import ExitStack

import concourse.bass as bass
import numpy as np
from concourse import mybir
from concourse.alu_op_type import AluOpType as ALU

F32 = mybir.dt.float32
BF16 = mybir.dt.bfloat16
F16 = mybir.dt.float16
I32 = mybir.dt.int32
U32 = mybir.dt.uint32
ACT = mybir.ActivationFunctionType
AX_X = mybir.AxisListType.X

P = 128
B, SEQ, FEAT, D = 8, 1024, 29, 128
HEADS, HD = 16, 32
HG = 4
GROUPS = HEADS // HG
QT = SEQ // P
POOL_HEADS = 3
CHUNK = 512
EPS = 1e-5
PARTS = 2
EXACT = 3 * HD
MAX_UNIT = 64.0

Q_STACK = (0, 1, 0)
K_STACK = (0, 0, 1)
RING = 4

UNITS = [(c, kt) for c in range(SEQ // CHUNK) for kt in range((c + 1) * CHUNK // P)]
PIECES = [(qt, tuple(range(h, h + n))) for qt in range(QT)
          for n in ((4, 4, 2, 2, 1, 1, 1, 1)[qt],) for h in range(0, HG, n)]
PIECE_SLOTS = {4: 3, 5: 4, 6: 4, 7: 4, 8: 3, 9: 2, 10: 2}


TOTAL1_AT = 0
VALUES_AT = 1
PROJECT_AT = 11
ROWS_AT = 10
TOTAL0_AT = 10
OUT_AT = 1
DEVIATE_AT = OUT_AT + 1
SCALE_AT = OUT_AT + 2


def pieces_at(u):
    first = sum(n for v, n in PIECE_SLOTS.items() if v < u)
    return PIECES[first:first + PIECE_SLOTS.get(u, 0)]


def unit_span(c, kt):
    q0 = max(CHUNK * c, P * kt)
    return q0, CHUNK * (c + 1) - q0


PROLOGUE_USES = (["fold0", "fold1", "bias", "outbias", "embed", "q", "k", "v"] + [("max",) + p for p in PIECES]
                 + ["rows", "q1", "k1"])


def iteration_uses(first, last):
    uses = []
    for g in range(GROUPS):
        one, two = not (last and g >= GROUPS - 1), not (last and g >= GROUPS - 2)
        for u in range(len(UNITS)):
            uses += [(g, ("max",) + p) for p in (pieces_at(u) if one else ())]
            if u == VALUES_AT and one:
                uses.append((g, "v"))
            if u == TOTAL1_AT and not (first and g == 0):
                uses.append((g - 1, "total1"))
            if u == OUT_AT and g == 0 and not first:
                uses.append((-1, "out"))
            if u == PROJECT_AT and two:
                uses += [(g, "embed")] * (g == GROUPS - 2) + [(g, "q"), (g, "k")]
            if u == ROWS_AT and one:
                uses.append((g, "rows"))
            if u == TOTAL0_AT:
                uses.append((g, "total0"))
    return uses + [(GROUPS - 1, "total1"), (GROUPS - 1, "out")] * last


def attention(nc, ins, h1, outer):
    ctx = outer.enter_context(ExitStack())

    def sb(name, shape, dt):
        return ctx.enter_context(nc.sbuf_tensor(name, shape, dt))

    def sem(name):
        return ctx.enter_context(nc.semaphore(name))

    wide = [ctx.enter_context(nc.psum_tensor(f"wide{i}", [P, SEQ], F32)) for i in range(2)]
    score = [ctx.enter_context(nc.psum_tensor(f"score{i}", [P, CHUNK], F32)) for i in range(2)]
    mixed = [ctx.enter_context(nc.psum_tensor(f"mixed{c}", [P, CHUNK], F32)) for c in range(2)]

    blT = sb("blT", [P, HEADS], F32)
    wqkv = sb("wqkv", [P, 3, HEADS * HD], F32)
    woT = sb("woT", [P, GROUPS, D], F32)
    bo = sb("bo", [P, D], F32)
    bias = sb("bias", [P, 3 * GROUPS], F32)
    wtok = sb("wtok", [FEAT, D], F32)
    cst = sb("cst", [P, 3, P], F32)
    ident = cst[:, 0, :]
    cst16 = sb("cst16", [P, 3, P], BF16)
    ident16, above, below = cst16[:, 0, :], cst16[:, 1, :], cst16[:, 2, :]
    ones = sb("ones", [P, HD], F32)
    peT = sb("peT", [P, SEQ], F32)
    peb = sb("peb", [P, QT, D], F32)

    x_next = sb("x_next", [FEAT, SEQ], F32)
    x_here = sb("x_here", [FEAT, SEQ], F32)
    h0T = sb("h0T", [P, SEQ], F32)
    parts = [sb(f"parts{i}", [P, PARTS, SEQ], F16) for i in range(2)]
    stack = [[sb(f"stack{p}{i}", [P, HG, SEQ], F16) for i in range(2)] for p in range(2)]
    values = [sb(f"values{p}", [P, QT, HG * HD], F32) for p in range(2)]
    probs = [sb(f"probs{i}", [P, HG, CHUNK], F32) for i in range(RING)]
    sums = [sb(f"sums{c}", [P, HG, CHUNK], F32) for c in range(2)]
    maxima = sb("maxima", [P, HG, QT], F32)
    neg_parts = sb("neg_parts", [HG * QT, PARTS, P], F16)
    recip = sb("recip", [P, CHUNK], F32)
    catT = sb("catT", [P, GROUPS, SEQ], F32)
    y = sb("y", [P, QT, D], F32)
    wl = catT[:, 0:2, :].rearrange("p g s -> p (g s)").rearrange("p (h d) -> p h d", h=HEADS)
    w3 = catT[:, 2:4, :].rearrange("p g s -> p (g s)")[:, 0:3 * HEADS * HD]\
        .rearrange("p (j h d) -> p j h d", j=3, h=HEADS)
    bv_wide = y[:, 0:GROUPS, :]
    stats = sb("stats", [P, QT, 6], F32)
    moments = sb("moments", [P, QT, 2], F32)
    rstd = sb("rstd", [P, QT], F32)
    eps = sb("eps", [P, 1], F32)

    passed = sem("passed")
    weights_loaded = sem("weights_loaded")
    consts_loaded = sem("consts_loaded")
    x_next_loaded = sem("x_next_loaded")
    x_here_loaded = sem("x_here_loaded")
    setup_done = sem("setup_done")
    bias_spread = sem("bias_spread")
    copied = sem("copied")
    wide_full = [sem(f"wide_full{i}") for i in range(2)]
    wide_free = [sem(f"wide_free{i}") for i in range(2)]
    rounded = sem("rounded")
    stacked = [sem(f"stacked{p}") for p in range(2)]
    rows_split = sem("rows_split")
    rows_stacked = sem("rows_stacked")
    score_full = sem("score_full")
    exponentials = sem("exponentials")
    mixes = sem("mixes")
    pool_sums = sem("pool_sums")
    dve_sums = sem("dve_sums")
    mixed_free = [sem(f"mixed_free{c}") for c in range(2)]
    moments_ready = sem("moments_ready")
    deviation = sem("deviation")
    rstd_ready = sem("rstd_ready")
    centred = sem("centred")
    normed = sem("normed")

    LOADS_W, LOADS_C = 8, 3
    SETUP_OPS = 7
    STACK_INC = 16 * HG * 2 * len(Q_STACK)
    ROWS_INC = 16 * PARTS
    uses = {(first, last): iteration_uses(first, last) for first, last in ((1, 0), (0, 0), (0, 1))}
    in_first, per_iter = len(uses[1, 0]), len(uses[0, 0])
    assert in_first % 2 == 0 and per_iter % 2 == 0

    def prologue_use(name):
        n = PROLOGUE_USES.index(name)
        return n % 2, n // 2

    def is_first(b):
        return isinstance(b, int) and b == 0

    def loop_use(b, g, name, last):
        n = len(PROLOGUE_USES) + uses[is_first(b), last].index((g, name))
        if is_first(b):
            return n % 2, n // 2
        return n % 2, b * (per_iter // 2) + (n + in_first - per_iter) // 2

    def image_of(b, g):
        return b if g == GROUPS - 1 else b - 1

    def using(b, g, name, last):
        return prologue_use(name) if b is None else loop_use(b, g, name, last)

    def wait_empty(eng, buf, k):
        eng.wait_ge(wide_free[buf], k)

    def wait_read(eng, buf, k):
        eng.wait_ge(wide_free[buf], k + 1)

    def operand(b, g, i):
        return "qk"[i] + ("1" if b is None and g == 1 else "")

    def ahead_of(b, g, step):
        if b is None:
            return g, g, g
        return GROUPS * b + g + step, (g + step) % GROUPS, (g + step) % 2

    def same_parity_before(b, g, step):
        return 0 if b is None else 2 * b + (g + step) // 2

    def add_up(eng, unit_engine, sem_done, b, g, u, h0, h1_):
        c, kt = UNITS[u]
        q0, w = unit_span(c, kt)
        n = GROUPS * b + g
        at = q0 - CHUNK * c
        src = probs[u % RING][:, h0:h1_, 0:w]
        dst = sums[c][:, h0:h1_, at:CHUNK]
        if kt == 0:
            return
        eng.wait_ge(exponentials, 2 + 48 * n + HG * u + h1_)
        if kt == 1:
            eng.wait_ge(mixed_free[c], n + 1)
            before = probs[(u - 1) % RING][:, h0:h1_, :]
            if at:
                eng.sem_inc(passed, 1)
                unit_engine.tensor_scalar(sums[c][:, h0:h1_, 0:at], before[:, :, 0:at], 1.0, None, ALU.mult)
            unit_engine.tensor_tensor(dst, before[:, :, at:CHUNK], src, ALU.add).then_inc(sem_done, 2)
        else:
            eng.wait_ge(sem_done, RING + 12 * n + u)
            unit_engine.tensor_tensor(dst, dst, src, ALU.add).then_inc(sem_done, 1)

    def looped(eng, body):
        body(0, False)
        with eng.Fori(1, B - 1) as b:
            body(b, False)
        body(B - 1, True)

    block = ctx.enter_context(nc.Block())

    @block.sync
    def _(sp):
        sp.dma_start(wl, ins["Wl"].rearrange("h o i -> o h i")).then_inc(weights_loaded, 16)
        for j, name in enumerate(("Wq", "Wk", "Wv")):
            sp.dma_start(w3[:, j], ins[name].rearrange("h o d -> o h d")).then_inc(weights_loaded, 16)
        sp.dma_start(blT[:], ins["blT"]).then_inc(weights_loaded, 16)
        sp.dma_start(woT[:], ins["WoT"].rearrange("(g p) d -> p g d", p=P)).then_inc(weights_loaded, 16)
        sp.dma_start(bo[:], ins["bo"].rearrange("(a d) -> a d", a=1).broadcast_to([P, D])).then_inc(weights_loaded, 16)
        sp.dma_start(wtok[:], ins["Wtok"]).then_inc(weights_loaded, 16)
        sp.dma_start(cst[:], ins["cst"]).then_inc(consts_loaded, 16)
        sp.dma_start(peT[:], ins["peT"]).then_inc(consts_loaded, 16)
        sp.dma_start(peb[:], ins["pe"].rearrange("(t p) d -> p t d", p=P)).then_inc(consts_loaded, 16)
        sp.dma_start(x_next[:], ins["xT"][0]).then_inc(x_next_loaded, 16)

        def stack_parts(b, g, last):
            n, _gm, par = ahead_of(b, g, 2)
            if b is not None:
                sp.wait_ge(score_full, 48 * (GROUPS * b + g + 1))
            for part in range(PARTS):
                for i, plan in enumerate((Q_STACK, K_STACK)):
                    if part == 0:
                        sp.wait_ge(rounded, 2 * n + i + 1)
                    else:
                        wait_read(sp, *using(b, g, operand(b, g, i), last))
                    for row in [r for r in range(len(plan)) if plan[r] == part]:
                        for h in range(HG):
                            sp.dma_start(stack[par][i][HD * row:HD * row + HD, h, :],
                                         parts[i][HD * h:HD * h + HD, part, :]).then_inc(stacked[par], 16)

        def stack_rows(b, g, last):
            n, _gm, par = ahead_of(b, g, 1)
            for part in range(PARTS):
                if part == 0:
                    sp.wait_ge(rows_split, n + 1)
                else:
                    wait_read(sp, *using(b, g, "rows", last))
                dst = stack[par][0][EXACT + part:EXACT + part + 1, :, :].rearrange("o h (t q) -> o (h t) q", q=P)
                sp.dma_start(dst, neg_parts[:, part, :]).then_inc(rows_stacked, 16)

        def x_of(b):
            return ins["xT"][bass.ds(b, 1)].rearrange("o f s -> (o f) s") if not isinstance(b, int) else ins["xT"][b]

        stack_parts(None, 0, False)
        stack_rows(None, 0, False)
        stack_parts(None, 1, False)

        def body(b, last):
            for g in range(GROUPS):
                if not (last and g == GROUPS - 1):
                    stack_rows(b, g, last)
                if not (last and g >= GROUPS - 2):
                    stack_parts(b, g, last)
                if g == 0 and not last:
                    sp.dma_start(x_next[:], x_of(b + 1)).then_inc(x_next_loaded, 16)
                if g == 1:
                    sp.dma_start(x_here[:], x_of(b)).then_inc(x_here_loaded, 16)

        looped(sp, body)

    @block.tensor
    def _(pe):
        pe.wait_ge(weights_loaded, 16 * LOADS_W)
        for half in range(2):
            buf, _k = prologue_use(f"fold{half}")
            for hh in range(8):
                h = 8 * half + hh
                for j in range(3):
                    o = wide[buf][:, 512 * (hh // 4) + 96 * (hh % 4) + HD * j:][:, 0:HD]
                    mm = nc.tensor.matmul(o, wl[:, h, :], w3[:, j, h, :], start=True, stop=True)
            mm.then_inc(wide_full[buf], 1)
        buf, k = prologue_use("bias")
        wait_empty(pe, buf, k)
        for j in range(3):
            for h in range(HEADS):
                hh, col = h % HG, j * GROUPS + h // HG
                mm = nc.tensor.matmul(wide[buf][HD * hh:HD * hh + HD, col:col + 1], w3[:, j, h, :],
                                      blT[:, h:h + 1], start=True, stop=True)
        mm.then_inc(wide_full[buf], 1)
        buf, k = prologue_use("outbias")
        wait_empty(pe, buf, k)
        pe.wait_ge(bias_spread, GROUPS)
        for g in range(GROUPS):
            mm = nc.tensor.matmul(wide[buf][:, 0:D], bv_wide[:, g, :], woT[:, g, :],
                                  start=(g == 0), stop=(g == GROUPS - 1))
        mm.then_inc(wide_full[buf], 1)
        pe.wait_ge(setup_done, SETUP_OPS)
        for half in range(2):
            wait_read(pe, *prologue_use(f"fold{half}"))

        def embed(b, g, last):
            buf, k = using(b, g, "embed", last)
            wait_empty(pe, buf, k)
            pe.wait_ge(x_next_loaded, 16 if b is None else 16 * (b + 2))
            for c in range(2):
                mm = nc.tensor.matmul(wide[buf][:, CHUNK * c:CHUNK * (c + 1)], wtok[:],
                                      x_next[:, CHUNK * c:CHUNK * (c + 1)], start=True, stop=True)
            mm.then_inc(wide_full[buf], 1)

        def project(b, g, j, last):
            name = "v" if j == 2 else operand(b, g, j)
            buf, k = using(b, g, name, last)
            _n, gm, _par = ahead_of(b, g, 1 if j == 2 else 2)
            if j == 0 and gm == 0:
                wait_read(pe, *using(b, g, "embed", last))
            wait_empty(pe, buf, k)
            w = wqkv[:, j, P * gm:P * (gm + 1)]
            if j < 2:
                for c in range(2):
                    mm = nc.tensor.matmul(wide[buf][:, CHUNK * c:CHUNK * (c + 1)], w,
                                          h0T[:, CHUNK * c:CHUNK * (c + 1)], start=True, stop=True)
            else:
                for t in range(QT):
                    mm = nc.tensor.matmul(wide[buf][:, P * t:P * (t + 1)], h0T[:, P * t:P * (t + 1)], w,
                                          start=True, stop=True)
            mm.then_inc(wide_full[buf], 1)

        def max_scores(b, g, piece, last):
            qt, heads = piece
            buf, k = using(b, g, ("max",) + piece, last)
            _n, _gm, par = ahead_of(b, g, 1)
            if piece == PIECES[0]:
                pe.wait_ge(stacked[par], STACK_INC * (1 + same_parity_before(b, g, 1)))
            wait_empty(pe, buf, k)
            qs, ks = stack[par]
            width = P * (qt + 1)
            for x, h in enumerate(heads):
                at = piece_column(qt, x)
                lhsT = qs[0:EXACT, h, P * qt:P * (qt + 1)]
                for k0 in range(0, width, CHUNK):
                    w = min(CHUNK, width - k0)
                    diagonal = k0 + w == width
                    nc.tensor.matmul(wide[buf][:, at + k0:at + k0 + w], lhsT, ks[0:EXACT, h, k0:k0 + w],
                                     start=True, stop=not diagonal)
                mm = nc.tensor.matmul(wide[buf][:, at + width - P:at + width], ident16, above,
                                      start=False, stop=True)
            mm.then_inc(wide_full[buf], 1)

        def turn_maxima(b, g, last):
            buf, k = using(b, g, "rows", last)
            wait_empty(pe, buf, k)
            wait_read(pe, *using(b, g, ("max",) + PIECES[-2], last))
            wait_read(pe, *using(b, g, ("max",) + PIECES[-1], last))
            nc.tensor.transpose(wide[buf][0:HG * QT, 0:P], maxima[:].rearrange("p h t -> p (h t)"), ident)\
              .then_inc(wide_full[buf], 1)

        def key_scores(b, g, u, h):
            c, kt = UNITS[u]
            q0, w = unit_span(c, kt)
            par, n = g % 2, GROUPS * b + g
            qs, ks = stack[par]
            e = score[h % 2]
            if u == 0 and h == 0:
                pe.wait_ge(rows_stacked, ROWS_INC * (n + 1))
            pe.wait_ge(exponentials, 48 * n + HG * u + h + 1)
            diagonal = P * kt >= CHUNK * c
            mm = nc.tensor.matmul(e[:, 0:w], ks[0:EXACT + PARTS, h, P * kt:P * (kt + 1)],
                                  qs[0:EXACT + PARTS, h, q0:q0 + w], start=True, stop=not diagonal)
            if diagonal:
                mm = nc.tensor.matmul(e[:, 0:P], ident16, below, start=False, stop=True)
            mm.then_inc(score_full, 1)

        def mix(b, g, u):
            c, kt = UNITS[u]
            q0, w = unit_span(c, kt)
            off = q0 - CHUNK * c
            n = GROUPS * b + g
            first, final = kt == 0, P * (kt + 1) == CHUNK * (c + 1)
            if first:
                pe.wait_ge(mixed_free[c], n + 1)
            pe.wait_ge(exponentials, 2 + 48 * n + HG * (u + 1))
            for h in range(HG):
                rows = slice(HD * h, HD * h + HD)
                mm = nc.tensor.matmul(mixed[c][rows, off:off + w], values[g % 2][:, kt, rows],
                                      probs[u % RING][:, h, 0:w], start=first, stop=final)
            mm.then_inc(mixes, 1)

        def total(b, g, c, last):
            n = GROUPS * b + g
            buf, k = loop_use(b, g, f"total{c}", last)
            wait_empty(pe, buf, k)
            pe.wait_ge(pool_sums, RING + 12 * n + (4, 12)[c])
            pe.wait_ge(dve_sums, RING + 12 * n + (4, 12)[c])
            for h in range(HG):
                mm = nc.tensor.matmul(wide[buf][HD * h:HD * h + HD, 0:CHUNK], ones[:], sums[c][:, h, :],
                                      start=True, stop=True)
            mm.then_inc(wide_full[buf], 1)

        def out_map(b, g, last):
            buf, k = loop_use(b, g, "out", last)
            image = image_of(b, g)
            wait_empty(pe, buf, k)
            pe.wait_ge(x_here_loaded, 16 * (image + 1))
            for t in range(QT):
                if P * t % CHUNK == 0:
                    pe.wait_ge(mixed_free[P * t // CHUNK], 1 + GROUPS * (image + 1))
                cols = slice(P * t, P * (t + 1))
                for gm in range(GROUPS):
                    nc.tensor.matmul(wide[buf][:, cols], catT[:, gm, cols], woT[:, gm, :], start=(gm == 0), stop=False)
                mm = nc.tensor.matmul(wide[buf][:, cols], x_here[:, cols], wtok[:], start=False, stop=True)
            mm.then_inc(wide_full[buf], 1)

        embed(None, 0, False)
        for j in range(3):
            project(None, 0, j, False)
        for piece in PIECES:
            max_scores(None, 0, piece, False)
        turn_maxima(None, 0, False)
        for j in range(2):
            project(None, 1, j, False)

        def body(b, last):
            for g in range(GROUPS):
                one, two = not (last and g >= GROUPS - 1), not (last and g >= GROUPS - 2)
                for u in range(len(UNITS)):
                    todo = list(pieces_at(u)) if one else []
                    for h in range(HG):
                        key_scores(b, g, u, h)
                        if todo:
                            max_scores(b, g, todo.pop(0), last)
                    if u >= 1:
                        mix(b, g, u - 1)
                    if u == VALUES_AT and one:
                        project(b, g, 2, last)
                    if u == TOTAL1_AT and not (is_first(b) and g == 0):
                        total(b, g - 1, 1, last)
                    if u == OUT_AT and g == 0 and not is_first(b):
                        out_map(b, -1, last)
                    if u == PROJECT_AT and two:
                        if g == GROUPS - 2:
                            embed(b, g, last)
                        project(b, g, 0, last)
                        project(b, g, 1, last)
                    if u == ROWS_AT and one:
                        turn_maxima(b, g, last)
                    if u == TOTAL0_AT:
                        total(b, g, 0, last)
                mix(b, g, len(UNITS) - 1)
            if last:
                total(b, GROUPS - 1, 1, last)
                out_map(b, GROUPS - 1, last)

        looped(pe, body)

    @block.scalar
    def _(act):
        for half in range(2):
            buf, k = prologue_use(f"fold{half}")
            act.wait_ge(wide_full[buf], k + 1)
            src = wide[buf][:].rearrange("p (a r) -> p a r", a=2)[:, :, 0:384]\
                .rearrange("p a (h j d) -> p a h j d", h=4, j=3)
            for j in range(3):
                for a in range(2):
                    dst = wqkv[:, j, 256 * half + 128 * a:256 * half + 128 * (a + 1)]
                    final = j == 2 and a == 1
                    nc.scalar.copy(dst.rearrange("p (h d) -> p h d", h=4), src[:, a, :, j, :])\
                      .then_inc(wide_free[buf] if final else copied, 1)

        def round_operand(b, g, i, last):
            buf, k = using(b, g, operand(b, g, i), last)
            n, gm, _par = ahead_of(b, g, 2)
            if b is not None or g == 1:
                before = (g + 1) % 2
                act.wait_ge(stacked[before], STACK_INC * (1 + (0 if b is None else same_parity_before(b, g, 1))))
            act.wait_ge(wide_full[buf], k + 1)
            bcol = bias[:, i * GROUPS + gm:i * GROUPS + gm + 1]
            nc.scalar.activation(parts[i][:, 0, :], wide[buf][:], ACT.Identity, bias=bcol).then_inc(rounded, 1)

        def copy_values(b, g, last):
            buf, k = using(b, g, "v", last)
            _n, _gm, par = ahead_of(b, g, 1)
            act.wait_ge(wide_full[buf], k + 1)
            nc.scalar.copy(values[par][:].rearrange("p t c -> p (t c)"), wide[buf][:]).then_inc(wide_free[buf], 1)

        def deviate(b, g):
            act.wait_ge(moments_ready, 2 * QT * (image_of(b, g) + 1))
            nc.scalar.activation(rstd[:], moments[:, :, 1], ACT.Sqrt, bias=eps[:, 0:1]).then_inc(deviation, 1)

        wait_read(act, *prologue_use("bias"))
        for i in range(2):
            round_operand(None, 0, i, False)
        copy_values(None, 0, False)
        for i in range(2):
            round_operand(None, 1, i, False)

        def body(b, last):
            for g in range(GROUPS):
                n = GROUPS * b + g
                one, two = not (last and g >= GROUPS - 1), not (last and g >= GROUPS - 2)
                for u in range(len(UNITS)):
                    _q0, w = unit_span(*UNITS[u])
                    act.wait_ge(mixes, 12 * n + u + 1)
                    act.wait_ge(pool_sums, 12 * n + u + 1)
                    act.wait_ge(dve_sums, 12 * n + u + 1)
                    for h in range(HG):
                        act.wait_ge(score_full, 48 * n + HG * u + h + 1)
                        nc.scalar.activation(probs[u % RING][:, h, 0:w], score[h % 2][:, 0:w], ACT.Exp)\
                          .then_inc(exponentials, 1)
                    if u == VALUES_AT and one:
                        copy_values(b, g, last)
                    if u == DEVIATE_AT and g == 0 and not is_first(b):
                        deviate(b, -1)
                    if u == PROJECT_AT and two:
                        round_operand(b, g, 0, last)
                        round_operand(b, g, 1, last)
            if last:
                deviate(b, GROUPS - 1)

        looped(act, body)

    @block.gpsimd
    def _(pool):
        def body(b, last):
            for g in range(GROUPS):
                for u in range(len(UNITS)):
                    add_up(pool, nc.gpsimd, pool_sums, b, g, u, 0, POOL_HEADS)

        looped(pool, body)

    @block.vector
    def _(dve):
        nc.vector.memset(ones[:], 1.0).then_inc(setup_done, 1)
        nc.vector.memset(eps[:], EPS).then_inc(setup_done, 1)
        nc.vector.memset(bv_wide, 0.0).then_inc(setup_done, 1)
        dve.sem_inc(exponentials, 2)
        for start_free in (mixes, pool_sums, dve_sums):
            dve.sem_inc(start_free, RING)
        for c in range(2):
            dve.sem_inc(mixed_free[c], 1)
        for par in range(2):
            nc.vector.memset(stack[par][1][EXACT:EXACT + PARTS, :, :], MAX_UNIT).then_inc(setup_done, 1)
        dve.wait_ge(consts_loaded, 16 * LOADS_C)
        nc.vector.tensor_copy(cst16[:], cst[:]).then_inc(setup_done, 1)
        buf, k = prologue_use("bias")
        dve.wait_ge(wide_full[buf], k + 1)
        nc.vector.tensor_copy(bias[:], wide[buf][:, 0:3 * GROUPS]).then_inc(wide_free[buf], 1)
        wait_read(dve, buf, k)
        dve.wait_ge(setup_done, 6)
        for g in range(GROUPS):
            nc.vector.tensor_scalar(bv_wide[:, g, :], bv_wide[:, g, :], bias[:, 2 * GROUPS + g:2 * GROUPS + g + 1],
                                    None, ALU.add).then_inc(bias_spread, 1)
        buf, k = prologue_use("outbias")
        dve.wait_ge(wide_full[buf], k + 1)
        dve.wait_ge(weights_loaded, 16 * LOADS_W)
        nc.vector.tensor_tensor(bo[:], bo[:], wide[buf][:, 0:D], ALU.add).then_inc(wide_free[buf], 1)
        wait_read(dve, buf, k)
        nc.vector.tensor_tensor(peb[:], peb[:], bo[:, None, :].broadcast_to([P, QT, D]), ALU.add)\
          .then_inc(setup_done, 1)
        dve.wait_ge(setup_done, SETUP_OPS)

        def add_positions(b, g, last):
            buf, k = using(b, g, "embed", last)
            dve.wait_ge(wide_full[buf], k + 1)
            nc.vector.tensor_tensor(h0T[:], wide[buf][:], peT[:], ALU.add).then_inc(wide_free[buf], 1)

        def low_part(b, g, i, last):
            buf, k = using(b, g, operand(b, g, i), last)
            n, gm, _par = ahead_of(b, g, 2)
            dve.wait_ge(rounded, 2 * n + i + 1)
            bcol = bias[:, i * GROUPS + gm:i * GROUPS + gm + 1]
            nc.vector.scalar_tensor_tensor(parts[i][:, 1, :], wide[buf][:], bcol, parts[i][:, 0, :], ALU.add,
                                           ALU.subtract).then_inc(wide_free[buf], 1)

        def piece_max(b, g, piece, last):
            qt, heads = piece
            buf, k = using(b, g, ("max",) + piece, last)
            width, n = P * (qt + 1), len(heads)
            dve.wait_ge(wide_full[buf], k + 1)
            if n == 4 and qt == 1:
                src = wide[buf][:].rearrange("p (h w) -> p h w", h=4)
            elif n == 4:
                src = wide[buf][:, 0:CHUNK].rearrange("p (h w) -> p h w", h=4)
            elif n == 2:
                src = wide[buf][:].rearrange("p (h w) -> p h w", h=2)[:, :, 0:width]
            else:
                src = wide[buf][:, None, 0:width]
            nc.vector.tensor_reduce(maxima[:, heads[0]:heads[0] + n, qt], src, AX_X, ALU.max)\
              .then_inc(wide_free[buf], 1)

        def split_maxima(b, g, last):
            buf, k = using(b, g, "rows", last)
            n = ahead_of(b, g, 1)[0]
            src = wide[buf][0:HG * QT, 0:P]
            dve.wait_ge(wide_full[buf], k + 1)
            if b is not None:
                dve.wait_ge(rows_stacked, ROWS_INC * n)
            nc.vector.tensor_scalar(neg_parts[:, 0, :], src, -1.0 / MAX_UNIT, None, ALU.mult).then_inc(rows_split, 1)
            dve.wait_ge(rows_split, n + 1)
            nc.vector.scalar_tensor_tensor(neg_parts[:, 1, :], src, -1.0 / MAX_UNIT, neg_parts[:, 0, :],
                                           ALU.mult, ALU.subtract).then_inc(wide_free[buf], 1)

        def normalise(b, g, c, last):
            n = GROUPS * b + g
            buf, k = loop_use(b, g, f"total{c}", last)
            dve.wait_ge(wide_full[buf], k + 1)
            nc.vector.reciprocal(recip[:], wide[buf][:, 0:CHUNK]).then_inc(wide_free[buf], 1)
            wait_read(dve, buf, k)
            nc.vector.tensor_tensor(catT[:, g % GROUPS, CHUNK * c:CHUNK * (c + 1)], mixed[c][:], recip[:], ALU.mult)\
              .then_inc(mixed_free[c], 1)

        def centre(b, g, last):
            buf, k = loop_use(b, g, "out", last)
            image = image_of(b, g)
            dve.wait_ge(wide_full[buf], k + 1)
            nc.vector.tensor_tensor(y[:].rearrange("p t d -> p (t d)"), wide[buf][:],
                                    peb[:].rearrange("p t d -> p (t d)"), ALU.add).then_inc(wide_free[buf], 1)
            wait_read(dve, buf, k)
            for t in range(QT):
                nc.vector.bn_stats(stats[:, t, :], y[:, t, :]).then_inc(moments_ready, 1)
            dve.wait_ge(moments_ready, 2 * QT * image + QT)
            dve.sem_inc(passed, 1)
            for t in range(QT):
                nc.vector.bn_aggr(moments[:, t, :], stats[:, t, :]).then_inc(moments_ready, 1)
            dve.wait_ge(moments_ready, 2 * QT * (image + 1))
            nc.vector.tensor_tensor(y[:], y[:], moments[:, :, 0:1].broadcast_to([P, QT, D]), ALU.subtract)\
              .then_inc(centred, 1)

        def scale(b, g):
            image = image_of(b, g)
            dve.wait_ge(deviation, image + 1)
            nc.vector.reciprocal(rstd[:], rstd[:]).then_inc(rstd_ready, 1)
            dve.wait_ge(centred, image + 1)
            dve.wait_ge(rstd_ready, image + 1)
            dst = h1[:, QT * image:QT * (image + 1), :] if isinstance(image, int) else h1[:, bass.ds(image * QT, QT), :]
            nc.vector.tensor_tensor(dst, y[:], rstd[:, :, None].broadcast_to([P, QT, D]), ALU.mult).then_inc(normed, 1)
            dve.wait_ge(normed, image + 1)

        add_positions(None, 0, False)
        for i in range(2):
            low_part(None, 0, i, False)
        for piece in PIECES:
            piece_max(None, 0, piece, False)
        split_maxima(None, 0, False)
        for i in range(2):
            low_part(None, 1, i, False)

        def body(b, last):
            for g in range(GROUPS):
                one, two = not (last and g >= GROUPS - 1), not (last and g >= GROUPS - 2)
                for u in range(len(UNITS)):
                    for piece in (pieces_at(u) if one else ()):
                        piece_max(b, g, piece, last)
                    if u >= 1:
                        add_up(dve, nc.vector, dve_sums, b, g, u - 1, POOL_HEADS, HG)
                    if u == TOTAL1_AT and not (is_first(b) and g == 0):
                        normalise(b, g - 1, 1, last)
                    if u == OUT_AT and g == 0 and not is_first(b):
                        centre(b, -1, last)
                    if u == SCALE_AT and g == 0 and not is_first(b):
                        scale(b, -1)
                    if u == PROJECT_AT and two:
                        if g == GROUPS - 2:
                            add_positions(b, g, last)
                        low_part(b, g, 0, last)
                        low_part(b, g, 1, last)
                    if u == ROWS_AT and one:
                        split_maxima(b, g, last)
                    if u == TOTAL0_AT:
                        normalise(b, g, 0, last)
                add_up(dve, nc.vector, dve_sums, b, g, len(UNITS) - 1, POOL_HEADS, HG)
            if last:
                normalise(b, GROUPS - 1, 1, last)
                centre(b, GROUPS - 1, last)
                scale(b, GROUPS - 1)

        looped(dve, body)

    return ctx


def piece_column(qt, x):
    return (P, 2 * P, CHUNK, CHUNK, 0, 0, 0, 0)[qt] * x


TILES = B * SEQ // P
KEYS, TOPK, FH = 64, 8, 8
EXPERTS = KEYS * KEYS
BLOCKS = EXPERTS // P
SLOTS = 2 * FH
CHOSEN = FH * TOPK
CANDS = 20
HALF = P // 2
BANK_PAIRS = CHUNK // (2 * BLOCKS)
BANKS = HALF // BANK_PAIRS
BIAS_PARTS = 3
SCALE = float(2 ** 14)
FLOOR = 12582912.0


def candidates(a, b, out):
    rows = lambda lo, hi, n: a[:, :, lo:hi, None].broadcast_to([P, FH, hi - lo, n])
    cols = lambda n, m: b[:, :, None, 0:n].broadcast_to([P, FH, m, n])
    at = lambda lo, m, n: out[:, :, lo:lo + m * n].rearrange("p h (m n) -> p h m n", m=m)
    return [(rows(0, 1, 8), cols(8, 1), at(0, 1, 8)), (rows(1, 2, 4), cols(4, 1), at(8, 1, 4)),
            (rows(2, 4, 2), cols(2, 2), at(12, 2, 2)), (rows(4, 8, 1), cols(1, 4), at(16, 4, 1))]


def feed_forward(nc, ins, h1, out, outer):
    ctx = outer.enter_context(ExitStack())

    def sb(name, shape, dt):
        return ctx.enter_context(nc.sbuf_tensor(name, shape, dt))

    def sem(name):
        return ctx.enter_context(nc.semaphore(name))

    def psum(name, shape):
        return ctx.enter_context(nc.psum_tensor(name, shape, F32))

    key_ps = psum("key_ps", [P, SLOTS * KEYS])
    turn_ps = psum("turn_ps", [P, CHUNK])
    inner_ps = psum("inner_ps", [P, 2, CHUNK])
    weight_ps = psum("weight_ps", [P, 2, CHUNK])
    up_ps = psum("up_ps", [P, CHUNK])

    down = sb("down", [P, BLOCKS, P], F32)
    up = sb("up", [P, BLOCKS, D], F32)
    wqT = up[0:KEYS, 0:SLOTS, :]
    keysT = up[0:KEYS, SLOTS:SLOTS + SLOTS // 2, :].rearrange("c a b -> c (a b)")\
        .rearrange("c (s n) -> c s n", s=SLOTS)
    bqT = up[0:KEYS, BLOCKS - 1, 0:SLOTS]
    wkey = sb("wkey", [P, SLOTS * KEYS], F32)
    bkey_row = sb("bkey_row", [1, BIAS_PARTS, SLOTS * KEYS], BF16)
    bkey_rest = sb("bkey_rest", [1, SLOTS * KEYS], F32)
    bkey = sb("bkey", [P, SLOTS * KEYS], BF16)
    ones16 = sb("ones16", [P, P], BF16)
    cst = sb("cst_ffn", [P, 2, P], F32)
    ident, iota = cst[:, 0, :], cst[:, 1, :]
    numbers = sb("numbers", [P, P, HALF], F16)
    eps = sb("eps_ffn", [P, 1], F32)

    xs = [sb(f"xs{i}", [P, D], F32) for i in range(2)]
    xT = [sb(f"xT{i}", [P, P], F32) for i in range(2)]
    keyscore = sb("keyscore", [P, SLOTS, KEYS], F32)
    tops = sb("tops", [P, FH, 2, TOPK], F32)
    ranks = sb("ranks", [P, FH, 2, TOPK], U32)
    ranksf = sb("ranksf", [P, FH, 2, TOPK], F32)
    cand = sb("cand", [P, FH, CANDS], F32)
    codes = sb("codes", [P, FH, CANDS], F32)
    best = sb("best", [P, FH, TOPK], F32)
    place = sb("place", [P, FH, TOPK], U32)
    placef = sb("placef", [P, FH, TOPK], F32)
    below_max = sb("below_max", [P, FH, TOPK], F32)
    expo = sb("expo", [P, FH, TOPK], F32)
    denom = sb("denom", [P, FH], F32)
    match = sb("match", [P, CANDS, CHOSEN], F32)
    expert = sb("expert", [P, CHOSEN], F32)
    choice = sb("choice", [P, 3, CHOSEN], F32)
    turned16 = sb("turned16", [P, 2, HALF], F16)
    weight16 = sb("weight16", [P, 2, HALF], F16)
    row_hot = sb("row_hot", [P, P, HALF], F16)
    block_hot = sb("block_hot", [P, BLOCKS, HALF], F16)
    sided = sb("sided", [P, 2, 2, BLOCKS, HALF], F16)
    vals = sb("vals", [P, BLOCKS, P], F32)
    stats = sb("stats_ffn", [P, 6], F32)
    moments = sb("moments_ffn", [P, 2], F32)
    rstd = sb("rstd_ffn", [P, 1], F32)
    result = [sb(f"result{i}", [P, D], F32) for i in range(2)]

    passed = sem("passed_ffn")
    small_loaded = sem("small_loaded")
    down_loaded = sem("down_loaded")
    up_loaded = sem("up_loaded")
    bias_loaded = sem("bias_loaded")
    ffn_setup = sem("ffn_setup")
    key_folded = sem("key_folded")
    key_copied = sem("key_copied")
    bias_parts = sem("bias_parts")
    x_copied = sem("x_copied")
    x_turned = sem("x_turned")
    xT_ready = sem("xT_ready")
    keys_scored = sem("keys_scored")
    keys_ready = sem("keys_ready")
    topped = sem("topped")
    summed = sem("summed")
    picked = sem("picked")
    coding = sem("coding")
    lowered = sem("lowered")
    matching = sem("matching")
    exponed = sem("exponed")
    deciding = sem("deciding")
    choices_turned = sem("choices_turned")
    turned_ready = sem("turned_ready")
    low_ready = sem("low_ready")
    built = sem("built")
    inner_full = sem("inner_full")
    rectified = sem("rectified")
    weight_full = sem("weight_full")
    weighted = sem("weighted")
    up_full = sem("up_full")
    moments_done = sem("moments_done")
    deviated = sem("deviated")
    inverted = sem("inverted")
    finished = sem("finished")
    stored = [sem(f"stored{i}") for i in range(2)]
    DECIDE, MATCH = 7, 4

    def looped(eng, body):
        with eng.Fori(0, TILES // 2 - 2) as pair:
            for par in range(2):
                body(2 * pair + par, pair, par, 3)
        for i in range(TILES - 4, TILES):
            body(i, i // 2, i % 2, min(3, TILES - 1 - i))

    block = ctx.enter_context(nc.Block())

    @block.sync
    def _(sp):
        sp.dma_start(wqT, ins["WqT_ffn"]).then_inc(small_loaded, 16)
        sp.dma_start(keysT, ins["keysT"]).then_inc(small_loaded, 16)
        sp.dma_start(bqT, ins["bqT"]).then_inc(small_loaded, 16)
        sp.dma_start(cst[:], ins["cst_ffn"]).then_inc(small_loaded, 16)
        sp.dma_start(down[:], ins["downT"].rearrange("d (n e) -> d n e", e=P)).then_inc(down_loaded, 16)
        sp.wait_ge(bias_parts, 4)
        for part in range(BIAS_PARTS):
            sp.dma_start(bkey[part:part + 1, :], bkey_row[:, part, :]).then_inc(bias_loaded, 16)
        sp.wait_ge(key_folded, 2)
        sp.dma_start(up[:], ins["up"].rearrange("(n e) d -> e n d", e=P)).then_inc(up_loaded, 16)

        def body(i, pair, par, ahead):
            sp.wait_ge(finished, i + 2)
            dst = out[bass.ds(i, 1)] if not isinstance(i, int) else out[i:i + 1]
            sp.dma_start(dst.rearrange("o p d -> (o p) d"), result[par][:]).then_inc(stored[par], 16)

        looped(sp, body)
        for par in range(2):
            sp.wait_ge(stored[par], 16 * (TILES // 2 + 1))

    @block.tensor
    def _(pe):
        pe.wait_ge(small_loaded, 16 * 4)
        for s in range(SLOTS):
            mm = nc.tensor.matmul(key_ps[:, KEYS * s:KEYS * (s + 1)], wqT[:, s, :], keysT[:, s, :],
                                  start=True, stop=True)
        mm.then_inc(key_folded, 1)
        flat = weight_ps[:].rearrange("p a b -> p (a b)")
        for s in range(SLOTS):
            mm = nc.tensor.matmul(flat[0:1, KEYS * s:KEYS * (s + 1)], bqT[:, s:s + 1], keysT[:, s, :],
                                  start=True, stop=True)
        mm.then_inc(key_folded, 1)
        pe.wait_ge(key_copied, 1)
        pe.wait_ge(ffn_setup, 5)
        pe.wait_ge(bias_loaded, 16 * BIAS_PARTS)

        def turn_tokens(j, par):
            pe.wait_ge(x_copied, j + 1)
            pe.wait_ge(keys_ready, j)
            nc.tensor.transpose(key_ps[:, 0:P], xs[par][:], ident).then_inc(x_turned, 1)

        def score_keys(j, par):
            pe.wait_ge(xT_ready, j + 1)
            for c in range(2):
                cols = slice(CHUNK * c, CHUNK * (c + 1))
                nc.tensor.matmul(key_ps[:, cols], xT[par][:], wkey[:, cols], start=True, stop=False)
                mm = nc.tensor.matmul(key_ps[:, cols], ones16[:], bkey[:, cols], start=False, stop=True)
            mm.then_inc(keys_scored, 1)

        def turn_choices(j):
            pe.wait_ge(deciding, DECIDE * (j + 1))
            pe.wait_ge(low_ready, j)
            for k in range(3):
                for side in range(2):
                    mm = nc.tensor.matmul(turn_ps[CHOSEN * side:CHOSEN * (side + 1), HALF * k:HALF * (k + 1)],
                                          choice[:, k, :], ident[:, HALF * side:HALF * (side + 1)],
                                          start=True, stop=True)
            mm.then_inc(choices_turned, 1)

        def inner(i, par):
            for k in range(BANKS):
                pe.wait_ge(rectified, BANKS * i + k + 1)
                for n in range(4 * k, 4 * k + 4):
                    mm = nc.tensor.matmul(inner_ps[:, k % 2, P * (n % 4):P * (n % 4 + 1)], down[:, n, :], xT[par][:],
                                          start=True, stop=True)
                mm.then_inc(inner_full, 1)

        def expert_weights(i, banks):
            for k in banks:
                if k % (BANKS // 2) == 0:
                    pe.wait_ge(built, 5 * i + 4 + k // (BANKS // 2))
                pe.wait_ge(weighted, BANKS * i + k + 1)
                for s in range(BANK_PAIRS):
                    t = BANK_PAIRS * k + s
                    for part in range(2):
                        mm = nc.tensor.matmul(weight_ps[:, k % 2, 2 * BLOCKS * s:2 * BLOCKS * (s + 1)],
                                              row_hot[:, :, t], sided[:, part, :, :, t],
                                              start=(part == 0), stop=(part == 1))
                mm.then_inc(weight_full, 1)

        def up_product(i):
            pe.wait_ge(weighted, 2 + BANKS * (i + 1))
            pe.wait_ge(finished, i + 1)
            here = h1[:, bass.ds(i, 1), :] if not isinstance(i, int) else h1[:, i:i + 1, :]
            nc.tensor.matmul(up_ps[:, 0:D], ident, here.rearrange("p o d -> p (o d)"), start=True, stop=False)
            for n in range(BLOCKS):
                mm = nc.tensor.matmul(up_ps[:, 0:D], vals[:, n, :], up[:, n, :],
                                      start=False, stop=(n == BLOCKS - 1))
            mm.then_inc(up_full, 1)

        for j in range(2):
            turn_tokens(j, j)
            score_keys(j, j)
        pe.wait_ge(down_loaded, 16)
        inner(0, 0)
        turn_choices(0)
        turn_tokens(2, 0)
        pe.wait_ge(up_loaded, 16)

        def body(i, pair, par, ahead):
            expert_weights(i, range(2))
            if ahead >= 2:
                score_keys(i + 2, par)
            expert_weights(i, range(2, BANKS))
            if ahead:
                turn_choices(i + 1)
            up_product(i)
            if ahead:
                inner(i + 1, 1 - par)
            if ahead == 3:
                turn_tokens(i + 3, 1 - par)

        looped(pe, body)

    @block.scalar
    def _(act):
        act.wait_ge(key_folded, 1)
        nc.scalar.copy(wkey[:], key_ps[:]).then_inc(key_copied, 1)

        def copy_tokens(j, par):
            act.wait_ge(x_turned, j + 1)
            nc.scalar.copy(xT[par][:], key_ps[:, 0:P]).then_inc(xT_ready, 1)

        def copy_keys(j):
            act.wait_ge(topped, 2 * j)
            act.wait_ge(keys_scored, j + 1)
            nc.scalar.copy(keyscore[:].rearrange("p s n -> p (s n)"), key_ps[:]).then_inc(keys_ready, 1)

        def exponentiate(j):
            act.wait_ge(lowered, j + 1)
            act.wait_ge(deciding, DECIDE * j)
            nc.scalar.activation(expo[:], below_max[:], ACT.Exp).then_inc(exponed, 1)

        def copy_choices(j):
            act.wait_ge(built, 5 * j)
            act.wait_ge(choices_turned, j + 1)
            nc.scalar.copy(turned16[:].rearrange("p a t -> p (a t)"), turn_ps[:, 0:2 * HALF]).then_inc(turned_ready, 1)
            nc.scalar.copy(weight16[:, 0, :], turn_ps[:, 2 * HALF:3 * HALF]).then_inc(turned_ready, 1)

        def rectify(i):
            for k in range(BANKS):
                act.wait_ge(inner_full, BANKS * i + k + 1)
                nc.scalar.activation(vals[:, 4 * k:4 * k + 4, :].rearrange("p n t -> p (n t)"), inner_ps[:, k % 2, :],
                                     ACT.Relu, scale=1.0 / SCALE).then_inc(rectified, 1)

        def deviate(i):
            act.wait_ge(moments_done, 2 * (i + 1))
            nc.scalar.activation(rstd[:], moments[:, 1:2], ACT.Sqrt, bias=eps[:, 0:1]).then_inc(deviated, 1)

        for j in range(2):
            copy_tokens(j, j)
            copy_keys(j)
        rectify(0)
        exponentiate(0)
        copy_choices(0)
        copy_tokens(2, 0)
        exponentiate(1)

        def body(i, pair, par, ahead):
            if ahead >= 2:
                copy_keys(i + 2)
            if ahead:
                copy_choices(i + 1)
                rectify(i + 1)
            if ahead >= 2:
                exponentiate(i + 2)
            if ahead == 3:
                copy_tokens(i + 3, 1 - par)
            deviate(i)

        looped(act, body)

    @block.gpsimd
    def _(pool):
        def copy_x(j, par, late):
            if late:
                pool.wait_ge(x_turned, j - 1)
                pool.sem_inc(passed, 1)
            src = h1[:, bass.ds(j, 1), :] if not isinstance(j, int) else h1[:, j:j + 1, :]
            nc.gpsimd.tensor_copy(xs[par][:, None, :], src).then_inc(x_copied, 1)

        def decode(j):
            pool.wait_ge(topped, 2 * (j + 1))
            pool.sem_inc(passed, 1)
            nc.gpsimd.tensor_copy(ranksf[:], ranks[:]).then_inc(coding, 1)
            pool.wait_ge(coding, 3 * j + 1)
            pool.sem_inc(passed, 1)
            nc.gpsimd.tensor_scalar(ranksf[:, :, 0, :], ranksf[:, :, 0, :], float(KEYS), None, ALU.mult)\
              .then_inc(coding, 1)
            pool.wait_ge(coding, 3 * j + 2)
            ops = candidates(ranksf[:, :, 0, :], ranksf[:, :, 1, :], codes)
            for a, b, o in ops:
                last = nc.gpsimd.tensor_tensor(o, a, b, ALU.add)
            last.then_inc(coding, 1)
            pool.wait_ge(picked, 2 * (j + 1))
            pool.wait_ge(exponed, j)
            nc.gpsimd.tensor_tensor(below_max[:], best[:], best[:, :, 0:1].broadcast_to([P, FH, TOPK]),
                                    ALU.subtract).then_inc(lowered, 1)
            nc.gpsimd.tensor_copy(placef[:], place[:]).then_inc(matching, 1)
            pool.wait_ge(matching, MATCH * j + 1)
            pool.wait_ge(deciding, DECIDE * j)
            pool.sem_inc(passed, 1)
            flat = placef[:].rearrange("p h k -> p (h k)")
            for c in range(CANDS):
                last = nc.gpsimd.tensor_scalar(match[:, c, :], flat, float(c), None, ALU.is_equal)
            last.then_inc(matching, 1)
            pool.wait_ge(matching, MATCH * j + 2)
            pool.wait_ge(coding, 3 * j + 3)
            view = match[:].rearrange("p c (h k) -> p c h k", h=FH)
            per_cand = codes[:].rearrange("p h c -> p c h")[:, :, :, None].broadcast_to([P, CANDS, FH, TOPK])
            nc.gpsimd.tensor_tensor(view, view, per_cand, ALU.mult).then_inc(matching, 1)
            pool.wait_ge(matching, MATCH * j + 3)
            nc.gpsimd.tensor_tensor(match[:, 0:CANDS // 2, :], match[:, 0:CANDS // 2, :], match[:, CANDS // 2:CANDS, :],
                                    ALU.add).then_inc(matching, 1)

        copy_x(0, 0, False)
        copy_x(1, 1, False)
        pool.wait_ge(ffn_setup, 5)
        decode(0)
        copy_x(2, 0, True)
        decode(1)

        def body(i, pair, par, ahead):
            if ahead == 3:
                copy_x(i + 3, 1 - par, True)
            if ahead >= 2:
                decode(i + 2)

        looped(pool, body)

    @block.vector
    def _(dve):
        dve.sem_inc(rectified, 2)
        dve.sem_inc(weighted, 2)
        dve.sem_inc(finished, 1)
        for par in range(2):
            dve.sem_inc(stored[par], 16)
        nc.vector.memset(ones16[:], 1.0).then_inc(ffn_setup, 1)
        nc.vector.memset(eps[:], EPS).then_inc(ffn_setup, 1)
        nc.vector.memset(bkey[:], 0.0).then_inc(ffn_setup, 1)
        dve.wait_ge(ffn_setup, 3)
        dve.wait_ge(small_loaded, 16 * 4)
        nc.vector.tensor_copy(numbers[:], iota[:, :, None].broadcast_to([P, P, HALF])).then_inc(ffn_setup, 1)
        dve.wait_ge(key_folded, 2)
        src = weight_ps[0:1, :, :].rearrange("p a b -> p (a b)")
        nc.vector.tensor_copy(bkey_row[:, 0, :], src).then_inc(bias_parts, 1)
        dve.wait_ge(bias_parts, 1)
        nc.vector.tensor_tensor(bkey_rest[:], src, bkey_row[:, 0, :], ALU.subtract).then_inc(bias_parts, 1)
        dve.wait_ge(bias_parts, 2)
        nc.vector.tensor_copy(bkey_row[:, 1, :], bkey_rest[:]).then_inc(bias_parts, 1)
        dve.wait_ge(bias_parts, 3)
        nc.vector.tensor_tensor(bkey_row[:, 2, :], bkey_rest[:], bkey_row[:, 1, :], ALU.subtract)\
          .then_inc(bias_parts, 1)
        dve.wait_ge(bias_parts, 4)
        nc.vector.memset(sided[:], 0.0).then_inc(ffn_setup, 1)
        dve.wait_ge(ffn_setup, 5)

        def search(j):
            dve.wait_ge(keys_ready, j + 1)
            dve.wait_ge(matching, MATCH * j)
            dve.sem_inc(passed, 1)
            for s in range(SLOTS):
                last = nc.vector.max(tops[:, s // 2, s % 2, :], keyscore[:, s, :])
            last.then_inc(topped, 1)
            dve.wait_ge(topped, 2 * j + 1)
            dve.sem_inc(passed, 1)
            for s in range(SLOTS):
                last = nc.vector.max_index(ranks[:, s // 2, s % 2, :], tops[:, s // 2, s % 2, :], keyscore[:, s, :])
            last.then_inc(topped, 1)
            for a, b, o in candidates(tops[:, :, 0, :], tops[:, :, 1, :], cand):
                last = nc.vector.tensor_tensor(o, a, b, ALU.add)
            last.then_inc(summed, 1)
            dve.wait_ge(summed, j + 1)
            dve.sem_inc(passed, 1)
            for h in range(FH):
                last = nc.vector.max(best[:, h, :], cand[:, h, :])
            last.then_inc(picked, 1)
            dve.wait_ge(picked, 2 * j + 1)
            dve.sem_inc(passed, 1)
            for h in range(FH):
                last = nc.vector.max_index(place[:, h, :], best[:, h, :], cand[:, h, :])
            last.then_inc(picked, 1)

        def decide(j, step):
            n = DECIDE * j
            if step == 0:
                dve.wait_ge(exponed, j + 1)
                nc.vector.tensor_reduce(denom[:], expo[:], AX_X, ALU.add).then_inc(deciding, 1)
            if step == 1:
                dve.wait_ge(matching, MATCH * (j + 1))
                nc.vector.tensor_reduce(expert[:], match[:, 0:CANDS // 2, :].rearrange("p c x -> p x c"), AX_X, ALU.add)\
                  .then_inc(deciding, 1)
            if step == 2:
                dve.wait_ge(deciding, n + 1)
                nc.vector.reciprocal(denom[:], denom[:]).then_inc(deciding, 1)
            if step == 3:
                dve.wait_ge(deciding, n + 2)
                dve.wait_ge(choices_turned, j)
                nc.vector.tensor_scalar(choice[:, 1, :], expert[:], 1.0 / P, 0.5 - 0.5 / P, ALU.mult, ALU.subtract)\
                  .then_inc(deciding, 1)
            if step == 4:
                dve.wait_ge(deciding, n + 3)
                nc.vector.scalar_tensor_tensor(choice[:, 2, :].rearrange("p (h k) -> p h k", h=FH), expo[:], SCALE,
                                               denom[:, :, None].broadcast_to([P, FH, TOPK]), ALU.mult, ALU.mult)\
                  .then_inc(deciding, 1)
            if step == 5:
                dve.wait_ge(deciding, n + 4)
                nc.vector.tensor_scalar(choice[:, 1, :], choice[:, 1, :], FLOOR, FLOOR, ALU.add, ALU.subtract)\
                  .then_inc(deciding, 1)
            if step == 6:
                dve.wait_ge(deciding, n + 6)
                nc.vector.scalar_tensor_tensor(choice[:, 0, :], choice[:, 1, :], -float(P), expert[:],
                                               ALU.mult, ALU.add).then_inc(deciding, 1)

        def low_parts(j):
            dve.wait_ge(turned_ready, 2 * (j + 1))
            nc.vector.tensor_tensor(weight16[:, 1, :], turn_ps[:, 2 * HALF:3 * HALF], weight16[:, 0, :],
                                    ALU.subtract).then_inc(low_ready, 1)

        def build_blocks(j):
            nc.vector.tensor_tensor(block_hot[:], numbers[:, 0:BLOCKS, :],
                                    turned16[:, 1, None, :].broadcast_to([P, BLOCKS, HALF]), ALU.is_equal)\
              .then_inc(built, 1)
            dve.wait_ge(low_ready, j + 1)
            dve.wait_ge(built, 5 * j + 1)
            for side in range(2):
                rows = slice(CHOSEN * side, CHOSEN * (side + 1))
                shape = [CHOSEN, 2, BLOCKS, HALF]
                nc.vector.tensor_tensor(sided[rows, :, side, :, :], block_hot[rows, None, :, :].broadcast_to(shape),
                                        weight16[rows, :, None, :].broadcast_to(shape), ALU.mult).then_inc(built, 1)

        def build_rows(half):
            cols = slice(HALF // 2 * half, HALF // 2 * (half + 1))
            nc.vector.tensor_tensor(row_hot[:, :, cols], numbers[:, :, cols],
                                    turned16[:, 0, None, cols].broadcast_to([P, P, HALF // 2]), ALU.is_equal)\
              .then_inc(built, 1)

        def weigh(i, k):
            dve.wait_ge(rectified, 2 + BANKS * i + BANKS)
            dve.wait_ge(weight_full, BANKS * i + k + 1)
            v = vals[:].rearrange("p n (s t) -> p s n t", s=2)[:, :, :, BANK_PAIRS * k:BANK_PAIRS * (k + 1)]
            nc.vector.tensor_tensor(v, weight_ps[:, k % 2, :].rearrange("p (t s n) -> p s n t", s=2, n=BLOCKS), v,
                                    ALU.mult).then_inc(weighted, 1)

        def moments_of(i):
            dve.wait_ge(up_full, i + 1)
            dve.sem_inc(passed, 1)
            nc.vector.bn_stats(stats[:], up_ps[:, 0:D]).then_inc(moments_done, 1)
            dve.wait_ge(moments_done, 2 * i + 1)
            dve.sem_inc(passed, 1)
            nc.vector.bn_aggr(moments[:], stats[:]).then_inc(moments_done, 1)

        def finish(i, pair, par):
            dve.wait_ge(deviated, i + 1)
            nc.vector.reciprocal(rstd[:], rstd[:]).then_inc(inverted, 1)
            dve.wait_ge(inverted, i + 1)
            dve.wait_ge(stored[par], 16 * (pair + 1))
            nc.vector.tensor_scalar(result[par][:], up_ps[:, 0:D], moments[:, 0:1], rstd[:, 0:1], ALU.subtract,
                                    ALU.mult)\
              .then_inc(finished, 1)

        def weigh_and_decide(i, ahead, finish_before):
            for k in range(BANKS):
                if ahead >= 1:
                    weigh(i + 1, k)
                if k == 1 and finish_before is not None:
                    finish(*finish_before)
                if ahead >= 2 and k < DECIDE:
                    decide(i + 2, k)

        search(0)
        for step in range(DECIDE):
            decide(0, step)
        search(1)
        low_parts(0)
        build_blocks(0)
        build_rows(0)
        build_rows(1)
        weigh_and_decide(-1, 3, None)

        def body(i, pair, par, ahead):
            if ahead >= 2:
                search(i + 2)
            if ahead:
                low_parts(i + 1)
                build_blocks(i + 1)
                build_rows(0)
            moments_of(i)
            if ahead:
                build_rows(1)
            weigh_and_decide(i, ahead, (i, pair, par))

        looped(dve, body)

    return ctx


def positions():
    position = np.arange(SEQ * 2, dtype=np.float32)[:, None]
    div_term = np.exp(np.arange(0, D, 2, dtype=np.float32) * (-np.log(10000.0) / D)).astype(np.float32)
    pe = np.zeros((SEQ * 2, D), dtype=np.float32)
    pe[:, 0::2] = np.sin(position * div_term)
    pe[:, 1::2] = np.cos(position * div_term)
    return pe[:SEQ]


FFN_INS = ["WqT_ffn", "keysT", "bqT", "cst_ffn", "downT", "up"]
ATT_INS = ["xT", "Wtok", "Wl", "blT", "Wq", "Wk", "Wv", "WoT", "bo", "pe", "peT", "cst"]


def host_arrays(**a):
    def lay(x):
        return np.ascontiguousarray(x)
    above = np.triu(np.full((P, P), -1e30, np.float32), 1)
    pe = positions()
    return {
        "xT": lay(np.asarray(a["x"]).reshape(B, SEQ, FEAT).transpose(0, 2, 1)),
        "Wtok": lay(a["L0_tok_W"]),
        "Wl": lay(a["L0_attn_Wl"]),
        "blT": lay(np.asarray(a["L0_attn_bl"]).T),
        "Wq": lay(a["L0_attn_Wq"]), "Wk": lay(a["L0_attn_Wk"]), "Wv": lay(a["L0_attn_Wv"]),
        "WoT": lay(np.asarray(a["L0_attn_Wo"]).T),
        "bo": lay(a["L0_attn_bo"]),
        "pe": pe, "peT": lay(pe.T),
        "WqT_ffn": lay(np.asarray(a["L0_ffn_Wq"]).reshape(D, SLOTS, KEYS).transpose(2, 1, 0)),
        "keysT": lay(np.asarray(a["L0_ffn_keys"]).reshape(SLOTS, KEYS, KEYS).transpose(2, 0, 1)),
        "bqT": lay(np.asarray(a["L0_ffn_bq"]).reshape(SLOTS, KEYS).T),
        "cst_ffn": lay(np.stack([np.eye(P, dtype=np.float32), np.tile(np.arange(P, dtype=np.float32), (P, 1))], 1)),
        "downT": lay(np.asarray(a["L0_ffn_w_down"]).T),
        "up": lay(a["L0_ffn_w_up"]),
        "cst": lay(np.stack([np.eye(P, dtype=np.float32), above, above.T], 1)),
    }


def vit_layer(nc, ins, out):
    with ExitStack() as ctx:
        h1 = ctx.enter_context(nc.sbuf_tensor("h1", [P, TILES, D], F32))
        with ExitStack() as first:
            attention(nc, ins, h1, first)
        with ExitStack() as second:
            feed_forward(nc, ins, h1, out, second)


def kernel(**inputs):
    import numpy as _np
    import concourse.bacc as _bacc
    from concourse import mybir as _mybir
    from concourse.bass_utils import run_bass_kernel_spmd as _run

    nc = _bacc.Bacc("TRN2", target_bir_lowering=False, num_devices=1)
    arrays, ins = {}, {}
    for name, a in host_arrays(**inputs).items():
        arrays[f"in_{name}_dram"] = a
        ins[name] = nc.dram_tensor(f"in_{name}_dram", a.shape, _mybir.dt.from_np(a.dtype), kind="ExternalInput").ap()
    out = nc.dram_tensor("out_dram", (TILES, P, D), _mybir.dt.float32, kind="ExternalOutput").ap()
    vit_layer(nc, ins, out)
    r = _run(nc, [arrays], core_ids=[0])
    return _np.asarray(r.results[0]["out_dram"]).reshape(B, SEQ, D)
```
